# Optimizing a Trainium2 kernel written in Bass

```python
import numpy as np
import jax
import jax.numpy as jnp

def _softmax(x, axis=-1):
    return jax.nn.softmax(x, axis=axis)

def _gelu(x):
    return jax.nn.gelu(x, approximate=True)

def _silu(x):
    return jax.nn.silu(x)

def _sigmoid(x):
    return jax.nn.sigmoid(x)

def _layernorm(x, axis=-1, eps=1e-05):
    m = jnp.mean(x, axis=axis, keepdims=True)
    v = jnp.var(x, axis=axis, keepdims=True)
    return (x - m) / jnp.sqrt(v + eps)

def _scatter_add(tgt, idx, src, axis=0):
    return tgt.at[idx].add(src)

def _segment_sum(src, seg, n):
    return jax.ops.segment_sum(src, seg, n)
kernel_name = 'mk_gnn_preln_d1_gnn_r64_5bf248'

def setup_inputs(seed: int=0):
    np.random.seed(seed)
    _w = jnp.asarray

    def _rec_inputs():
        import jax
        import jax.numpy as jnp
        _gk = jax.random.key(seed)
        x = -0.0002117 + 1 * jax.random.normal(jax.random.fold_in(_gk, 1), (50000, 256), jnp.float32)
        src = jax.random.randint(jax.random.fold_in(_gk, 2), (25000,), 0, 50000, jnp.int32)
        dst = jnp.minimum((50000 * jax.random.uniform(jax.random.fold_in(_gk, 3), (25000,)) ** 2.0).astype(jnp.int32), 49999)
        _o = jnp.argsort(dst, stable=True)
        src = src[_o]
        dst = dst[_o]
        edge_weight = jax.random.uniform(jax.random.fold_in(_gk, 12), (25000,), jnp.float32, 0.0, 0.999998)
        edge_weight_n2 = jax.random.uniform(jax.random.fold_in(_gk, 13), (25000,), jnp.float32, 0.0, 0.999998)
        return (x, src, dst, edge_weight, edge_weight_n2)
    x, src, dst, edge_weight, edge_weight_n2 = _rec_inputs()

    def _L0_gnn_setup():
        import jax, jax.numpy as jnp
        import numpy as np
        N_NODES = 100000
        N_EDGES = 12500
        DIM = 256
        EPS = 1e-05
        key = jax.random.key(seed)
        ks = jax.random.split(key, 12)
        H = DIM
        s = 1.0 / np.sqrt(H)
        s2 = 1.0 / np.sqrt(2 * H)
        return {'feat': jax.random.normal(ks[0], (N_NODES, DIM), dtype=jnp.float32), 'src': jax.random.randint(ks[1], (N_EDGES,), 0, N_NODES, dtype=jnp.int32), 'dst': jax.random.randint(ks[2], (N_EDGES,), 0, N_NODES, dtype=jnp.int32), 'iw': jax.random.uniform(ks[3], (N_EDGES,), dtype=jnp.float32), 'ow': jax.random.uniform(ks[4], (N_EDGES,), dtype=jnp.float32), 'gamma': jnp.ones((DIM,), jnp.float32), 'beta': jnp.zeros((DIM,), jnp.float32), 'W_in': jax.random.uniform(ks[5], (H, H), jnp.float32, -s, s), 'b_in': jax.random.uniform(ks[6], (H,), jnp.float32, -s, s), 'W_out': jax.random.uniform(ks[7], (H, H), jnp.float32, -s, s), 'b_out': jax.random.uniform(ks[8], (H,), jnp.float32, -s, s), 'W_x2i': jax.random.uniform(ks[9], (2 * H, 2 * H), jnp.float32, -s2, s2), 'b_x2i': jax.random.uniform(ks[10], (2 * H,), jnp.float32, -s2, s2), 'W_h2h': jax.random.uniform(ks[11], (H, 2 * H), jnp.float32, -s, s)}
    _L0_gnn_all = _L0_gnn_setup()
    _L0_gnn_in = {k: v for k, v in _L0_gnn_all.items() if k in ('gamma', 'beta', 'W_in', 'b_in', 'W_out', 'b_out', 'W_x2i', 'b_x2i', 'W_h2h')}
    del _L0_gnn_all
    return {'x': x, 'src': src, 'dst': dst, 'edge_weight': edge_weight, 'edge_weight_n2': edge_weight_n2, 'L0_gnn_gamma': _L0_gnn_in['gamma'], 'L0_gnn_beta': _L0_gnn_in['beta'], 'L0_gnn_W_in': _L0_gnn_in['W_in'], 'L0_gnn_b_in': _L0_gnn_in['b_in'], 'L0_gnn_W_out': _L0_gnn_in['W_out'], 'L0_gnn_b_out': _L0_gnn_in['b_out'], 'L0_gnn_W_x2i': _L0_gnn_in['W_x2i'], 'L0_gnn_b_x2i': _L0_gnn_in['b_x2i'], 'L0_gnn_W_h2h': _L0_gnn_in['W_h2h']}

def reference(x, src, dst, edge_weight, edge_weight_n2, L0_gnn_gamma, L0_gnn_beta, L0_gnn_W_in, L0_gnn_b_in, L0_gnn_W_out, L0_gnn_b_out, L0_gnn_W_x2i, L0_gnn_b_x2i, L0_gnn_W_h2h):
    import jax
    import jax.numpy as jnp

    def _L0_gnn_ref(feat, src, dst, iw, ow, gamma, beta, W_in, b_in, W_out, b_out, W_x2i, b_x2i, W_h2h):
        import jax, jax.numpy as jnp
        import numpy as np
        N_NODES = 100000
        N_EDGES = 12500
        DIM = 256
        EPS = 1e-05
        N = feat.shape[0]
        num_steps = 1
        mean = jnp.mean(feat, axis=0)
        var = jnp.var(feat, axis=0)
        h = (feat - mean) * jax.lax.rsqrt(var + EPS) * gamma + beta
        for _ in range(num_steps):
            feat_in = h @ W_in + b_in
            feat_out = h @ W_out + b_out
            a_in = jax.ops.segment_sum(feat_in[src] * iw[:, None], dst, num_segments=N)
            a_out = jax.ops.segment_sum(feat_out[dst] * ow[:, None], src, num_segments=N)
            a = jnp.concatenate((a_in, a_out), axis=1)
            xi = a @ W_x2i + b_x2i
            hh = h @ W_h2h
            i_i, i_n = jnp.split(xi, 2, axis=1)
            h_i, h_n = jnp.split(hh, 2, axis=1)
            input_gate = jax.nn.sigmoid(i_i + h_i)
            new_gate = jnp.tanh(i_n + h_n)
            h = new_gate + input_gate * (h - new_gate)
        return h
    h = jnp.maximum(_layernorm(x, axis=-1), 0.0)
    x = x + _L0_gnn_ref(h, src, dst, edge_weight, edge_weight_n2, L0_gnn_gamma, L0_gnn_beta, L0_gnn_W_in, L0_gnn_b_in, L0_gnn_W_out, L0_gnn_b_out, L0_gnn_W_x2i, L0_gnn_b_x2i, L0_gnn_W_h2h)
    return x

_drawn_inputs = setup_inputs


def setup_inputs(seed=0):
    import zlib

    import numpy as np

    out = dict(_drawn_inputs(seed))
    spreads = {'L0_gnn_gamma': (1.0, 0.2), 'L0_gnn_beta': (0.0, 0.1)}
    factors = {'edge_weight': 3.547,
     'edge_weight_n2': 3.508,
     'L0_gnn_b_in': 8.0,
     'L0_gnn_b_out': 8.0,
     'L0_gnn_b_x2i': 6.216}
    for name, (base, spread) in spreads.items():
        noise = np.random.default_rng([zlib.crc32(name.encode()), seed]).standard_normal(out[name].shape)
        drawn = base * np.exp(spread * noise) if base else spread * noise
        out[name] = jnp.asarray(drawn.astype(out[name].dtype))
    for name, factor in factors.items():
        out[name] = (out[name] * factor).astype(out[name].dtype)
    return out
```

```python
from contextlib import ExitStack

import concourse.bass as bass
from concourse import mybir
import numpy as np

F32 = mybir.dt.float32
F32R = mybir.dt.float32r
I32 = mybir.dt.int32
U32 = mybir.dt.uint32
ALU = mybir.AluOpType
ACT = mybir.ActivationFunctionType

P = 128
EPS = 1e-5
SLOTS = 4
IN, OUT = 0, 1


def value(engine, n):
    return n if isinstance(n, int) else engine.to_reg(n)


def before(engine, sem, step, lag, per=1):
    if not (isinstance(step, int) and step < lag):
        engine.wait_ge(sem, (step - lag + 1) * per)


def build(nc, x, src, dst, w_in_edge, w_out_edge, gamma, beta, W_in, b_in, W_out, b_out, W_x2i, b_x2i, W_h2h, out):
    N, D = x.shape
    E = src.shape[0]
    H2 = W_h2h.shape[1]
    KC = D // P
    ROWS = 4
    GROUP = P * ROWS
    FULL = N // GROUP
    REST = N - FULL * GROUP
    REST_ROWS = -(-REST // P)
    REST_P = REST // REST_ROWS
    GROUPS = FULL + 1
    BODIES = FULL // SLOTS
    assert 0 < REST and REST % (16 * REST_ROWS) == 0 and FULL - BODIES * SLOTS == 1 and KC == 2 and H2 == 2 * D
    TILES = -(-E // P)
    LAST_E = E - (TILES - 1) * P
    assert TILES % SLOTS == 0 and P < TILES <= 2 * P and 0 < LAST_E < P
    DUMMY = N
    PAD_ROW = N + 2 * P
    PRE_PER_P = -(-(PAD_ROW + 1) // P)
    PRE_ROWS = PRE_PER_P * P
    CLEARS = 4 * BODIES
    CLEAR = PRE_PER_P // CLEARS
    CLEARS_AHEAD = 2
    REST_CLEARS = [(r, min(CLEAR, PRE_PER_P - r)) for r in range(CLEARS * CLEAR, PRE_PER_P, CLEAR)]
    assert CLEARS % CLEARS_AHEAD == 0

    pre = nc.dram_tensor("pre_gates", [PRE_ROWS, H2], F32).ap()
    pre_by_p = pre.rearrange("(p r) f -> p (r f)", p=P)

    x_full = x[0:FULL * GROUP, :].rearrange("(g p r) f -> p g (r f)", p=P, r=ROWS)
    x_rest = x[FULL * GROUP:N, :].rearrange("(p r) f -> p (r f)", r=REST_ROWS)
    out_full = out[0:FULL * GROUP, :].rearrange("(g p r) f -> p g (r f)", p=P, r=ROWS)
    out_rest = out[FULL * GROUP:N, :].rearrange("(p r) f -> p (r f)", r=REST_ROWS)
    pre_full = pre[0:FULL * GROUP, :].rearrange("(g p r) f -> p g (r f)", p=P, r=ROWS)
    pre_rest = pre[FULL * GROUP:N, :].rearrange("(p r) f -> p (r f)", r=REST_ROWS)

    ctx = ExitStack()
    with ctx:
        def sb(name, shape, dt=F32):
            return ctx.enter_context(nc.sbuf_tensor(name, shape, dt))

        def sem(name):
            return ctx.enter_context(nc.semaphore(name))

        ident = sb("ident", [P, P])
        earlier = sb("earlier", [P, P])
        ones = sb("ones", [P, P])
        ones_r = sb("ones_r", [2, P], F32R)
        dummy_rows = sb("dummy_rows", [P, 2])
        iota_i = sb("iota_i", [P, 2], I32)
        eps_col = sb("eps_col", [P, 1])
        row_masks = sb("row_masks", [P, 4])
        edge_rows_i = sb("edge_rows_i", [P, 2, 2, P], I32)
        edge_rows = sb("edge_rows", [P, 4, 2, P])
        edge_cols = sb("edge_cols", [P, TILES, 4])
        gather_cols = sb("gather_cols", [P, TILES, 2], U32)
        Wx = sb("Wx", [P, 2, KC, H2])
        Wh = sb("Wh", [P, KC, H2])
        bmsg = sb("bmsg", [P, 2, KC])
        bx_row = sb("bx_row", [1, H2])
        gb = sb("gb", [P, 2, KC])
        M = sb("M", [P, 2, KC, H2])
        M_hi = sb("M_hi", [P, 2, KC, H2], F32R)
        M_lo = sb("M_lo", [P, 2, KC, H2], F32R)
        Wh_hi = sb("Wh_hi", [P, KC, H2], F32R)
        Wh_lo = sb("Wh_lo", [P, KC, H2], F32R)
        col4 = sb("col4", [P, 3, KC, 4])
        vec4_hi = sb("vec4_hi", [4, H2], F32R)
        const4 = sb("const4", [4, 3, H2], F32R)
        bn_mv = sb("bn_mv", [P, KC, 2])
        bn_std = sb("bn_std", [P, KC])
        bn_rstd = sb("bn_rstd", [P, KC])
        bn_t = sb("bn_t", [P, KC])
        bn_A = sb("bn_A", [P, KC])
        bn_C = sb("bn_C", [P, KC])
        rep = sb("rep", [P, 2, KC, P])
        A_rows = sb("A_rows", [P, 2, D])
        C_rows = sb("C_rows", [P, 2, D])
        xs = sb("xs", [P, SLOTS, ROWS, D])
        hs = sb("hs", [P, SLOTS, ROWS, D])
        Wmsg = hs[:, 0].rearrange("p (d c) n -> p d c n", d=2)
        WmsgT = hs[:, 1].rearrange("p (d c) n -> p d c n", d=2)
        spare = [xs[:, k].rearrange("p r f -> p (r f)")[:, 0:H2] for k in range(3)]
        scaled, vec4, vec4_lo = spare[0], spare[1][0:4, :], spare[2][0:4, :]
        ln_stats = sb("ln_stats", [P, SLOTS, ROWS, 6])
        ln_mv = sb("ln_mv", [P, SLOTS, ROWS, 2])
        ln_std = sb("ln_std", [P, SLOTS, ROWS])
        ln_r = sb("ln_r", [P, GROUPS, ROWS])
        ln_b = sb("ln_b", [P, GROUPS, ROWS])
        col_stats = sb("col_stats", [P, KC, GROUPS, 6])
        gidx = sb("gidx", [P, SLOTS, 2], U32)
        xg = [[sb(f"xg_{d}_{b}", [P, D]) for b in range(SLOTS)] for d in range(2)]
        g = sb("g", [P, SLOTS, 2, D])
        e_stats = sb("e_stats", [P, SLOTS, 2, 6])
        e_mv = sb("e_mv", [P, SLOTS, 2, 2])
        e_std = sb("e_std", [P, SLOTS, 2])
        e_r = sb("e_r", [P, SLOTS, 2])
        e_b = sb("e_b", [P, SLOTS, 2])
        cols = sb("cols", [P, SLOTS, 4])
        merge = sb("merge", [P, SLOTS, 2, P])
        cross = sb("cross", [P, SLOTS, P])
        junk = sb("junk", [P, 2, P])
        dups = sb("dups", [P, SLOTS, 2])
        shift = sb("shift", [P, SLOTS, 2])
        kept = sb("kept", [P, SLOTS, 2])
        rows_f = sb("rows_f", [P, SLOTS, 2])
        moved = sb("moved", [P, SLOTS, 1])
        moved2 = sb("moved2", [P, SLOTS, 1])
        taken = sb("taken", [P, SLOTS, 1])
        rows_u = [[sb(f"rows_u_{d}_{b}", [P, 1], U32) for b in range(SLOTS)] for d in range(2)]
        gT_hi = sb("gT_hi", [P, SLOTS, 2, KC, P], F32R)
        gT_lo = sb("gT_lo", [P, SLOTS, 2, KC, P], F32R)
        s_hi = sb("s_hi", [4, SLOTS, 2, P], F32R)
        s4 = sb("s4", [4, SLOTS, 2, P], F32R)
        pres = sb("pres", [P, SLOTS, ROWS, H2])
        pres_flat = pres[:, :, :, :].rearrange("p b r f -> p (b r f)")
        zeros = pres_flat[:, 0:CLEAR * H2]
        NEW = pres_flat.shape[1] - 2 * SLOTS * H2
        assert CLEAR * H2 <= NEW
        pre_new = [[pres_flat[:, NEW + (d * SLOTS + b) * H2:NEW + (d * SLOTS + b + 1) * H2] for b in range(SLOTS)] for d in range(2)]
        results = [g[:, 2 * k:2 * k + 2].rearrange("p b d f -> p (b d) f") for k in range(2)]
        hT_hi, hT_lo = gT_hi, gT_lo

        bank = [ctx.enter_context(nc.psum_tensor(f"bank{i}", [P, 512], F32)) for i in range(8)]
        hT_ps1 = [[bank[2 * s + c] for c in range(KC)] for s in range(SLOTS)]
        idx_ps = [bank[s][:, 0:2 * P].rearrange("p (d r) -> p d r", d=2) for s in range(2)]
        s_ps = [bank[s][0:4, 2 * P:4 * P] for s in range(2)]
        gT_ps = [bank[2 + s][:, :].rearrange("p (d c r) -> p d c r", d=2, c=KC) for s in range(2)]
        pre_ps = [[bank[4 + 2 * d + s] for s in range(2)] for d in range(2)]
        hT_ps3 = [bank[s][:, :].rearrange("p (j c r) -> p j c r", j=2, c=KC) for s in range(4)]
        node_ps = [bank[4 + j] for j in range(4)]

        def sems(names):
            return [sem(name) for name in names.split()]

        pool_const, pool_self, pads_set, edges_in, weights_in = sems("pool_const pool_self pads_set edges_in weights_in")
        dve_self, rows_ready, edgeT_ready, edge_tables = sems("dve_self rows_ready edgeT_ready edge_tables")
        WT_ready, WT_saved, M_ready, M_saved = sems("WT_ready WT_saved M_ready M_saved")
        x_in = [sem(f"x_in_{b}") for b in range(SLOTS)]
        zeros_set = sem("zeros_set")
        rest_cleared = sem("rest_cleared")
        pre_cleared = [sem(f"pre_cleared_{k}") for k in range(CLEARS_AHEAD)]
        stats_ready, var_ready, std_ready, rstd_ready, ln_ready = sems("stats_ready var_ready std_ready rstd_ready ln_ready")
        h_ready, hT_ready, hT_used = sems("h_ready hT_ready hT_used")
        bn_var, bn_std_ready, bn_cols_ready, vec_ready, rows_T, weights_ready = sems(
            "bn_var bn_std_ready bn_cols_ready vec_ready rows_T weights_ready")
        gathered = [sem(f"gathered_{b}") for b in range(SLOTS)]
        gidx_ready, cols_ready, idxT_ready = sems("gidx_ready cols_ready idxT_ready")
        estats_ready, evar_ready, estd_ready, erstd_ready, eln_ready, g_ready = sems(
            "estats_ready evar_ready estd_ready erstd_ready eln_ready g_ready")
        merge_ready, dups_ready, kept_ready, rows_ready2, cross_ready, moved_ready, moved2_ready, rows_u_ready = sems(
            "merge_ready dups_ready kept_ready rows_ready2 cross_ready moved_ready moved2_ready rows_u_ready")
        gT_ready, gT_hi_ready, gT_lo_ready = sems("gT_ready gT_hi_ready gT_lo_ready")
        pre_in_ready, pre_in_saved, projected, pre_out_ready, pre_out_saved, scattered = sems(
            "pre_in_ready pre_in_saved projected pre_out_ready pre_out_saved scattered")
        x3_in = [sem(f"x3_in_{b}") for b in range(SLOTS)]
        pre_in = [sem(f"pre_in_{b}") for b in range(SLOTS)]
        out_stored = [sem(f"out_stored_{b}") for b in range(2)]
        h3_ready, h3T_ready, h3T_hi, h3T_lo, own_ready, gates_in, gates_ready = sems(
            "h3_ready h3T_ready h3T_hi h3T_lo own_ready gates_in gates_ready")
        bn_scaled, bn_h_ready, diff_ready, gated_ready, mixed, summed = sems(
            "bn_scaled bn_h_ready diff_ready gated_ready mixed summed")

        block = ctx.enter_context(nc.Block())

        def size(group):
            return (REST_P, REST_ROWS) if isinstance(group, int) and group == GROUPS - 1 else (P, ROWS)

        def over_groups(engine, step):
            for b in range(SLOTS):
                step(b, 0, b)
            with engine.Fori(1, BODIES) as i:
                for b in range(SLOTS):
                    step(i * SLOTS + b, i, b)
            for group in range(BODIES * SLOTS, GROUPS):
                step(group, BODIES, group % SLOTS)

        def over_groups3(engine, step):
            for b in range(SLOTS):
                step(b, 0, b)
            with engine.Fori(1, BODIES - 1) as i:
                for b in range(SLOTS):
                    step(i * SLOTS + b, i, b)
            for group in range((BODIES - 1) * SLOTS, GROUPS):
                step(group, group // SLOTS, group % SLOTS)

        def over_tiles(engine, step):
            for t in range(2 * SLOTS):
                step(t, t // SLOTS, t % SLOTS)
            with engine.Fori(2, TILES // SLOTS - 1) as i:
                for b in range(SLOTS):
                    step(i * SLOTS + b, i, b)
            for t in range(TILES - SLOTS, TILES):
                step(t, t // SLOTS, t % SLOTS)

        def over_pairs(engine, step):
            for group in range(SLOTS):
                for q in range(2):
                    step(Pair(group, 0, group, q))
            with engine.Fori(1, BODIES - 1) as i:
                for b in range(SLOTS):
                    for q in range(2):
                        step(Pair(i * SLOTS + b, i, b, q))
            for group in range((BODIES - 1) * SLOTS, GROUPS):
                for q in range(2):
                    step(Pair(group, group // SLOTS, group % SLOTS, q))

        class Pair:

            def __init__(self, group, turn, slot, q):
                self.group, self.turn, self.slot, self.q = group, turn, slot, q
                self.parts, rows = size(group)
                self.j0, self.j1 = 2 * q, min(2 * q + 2, rows)
                self.rows = self.j1 - self.j0
                self.index = group * 2 + q
                self.buf = (2 * slot + q) % 4
                self.there = not isinstance(group, int) or 0 <= group < GROUPS

            def shifted(self, k):
                groups, q = divmod(self.q + k, 2)
                turns, slot = divmod(self.slot + groups, SLOTS)
                return Pair(self.group + groups, self.turn + turns, slot, q)

        LAST = Pair(GROUPS - 1, (GROUPS - 1) // SLOTS, (GROUPS - 1) % SLOTS, 1)

        def is_first(step):
            return isinstance(step, int) and step == 0

        def flat(ap):
            return ap.rearrange("p r f -> p (r f)")

        @block.sync
        def _(sp):
            sp.wait_ge(pads_set, 2)
            tail = TILES - 1 - P
            for a, rows in ((dst, edge_rows_i[:, 0]), (src, edge_rows_i[:, 1]),
                            (w_in_edge, edge_rows[:, 2]), (w_out_edge, edge_rows[:, 3])):
                sp.dma_start(rows[:, 0, :], a[0:P * P].rearrange("(t e) -> t e", e=P)).then_inc(edges_in, 16)
                sp.dma_start(rows[0:tail, 1, :],
                             a[P * P:(TILES - 1) * P].rearrange("(t e) -> t e", e=P)).then_inc(edges_in, 16)
                sp.dma_start(rows[tail:tail + 1, 1, 0:LAST_E],
                             a[(TILES - 1) * P:E].rearrange("(t e) -> t e", t=1)).then_inc(edges_in, 16)

            def load1(group, turn, b):
                before(sp, h_ready, group, SLOTS)
                n_p, n_r = size(group)
                if n_p == P:
                    sp.dma_start(flat(xs[:, b]), x_full[:, bass.ds(group, 1), :].rearrange("p a f -> p (a f)")).then_inc(x_in[b], 16)
                else:
                    sp.dma_start(flat(xs[0:n_p, b, 0:n_r]), x_rest).then_inc(x_in[b], 16)

            over_groups(sp, load1)

            sp.wait_ge(h_ready, GROUPS)
            sp.wait_ge(scattered, 32 * TILES)

            def load3(what, group, b):
                n_p, n_r = size(group)
                rows, full, rest, loaded = (xs, x_full, x_rest, x3_in) if what == "x" else (pres, pre_full, pre_rest, pre_in)
                if n_p == P:
                    sp.dma_start(flat(rows[:, b]), full[:, bass.ds(group, 1), :].rearrange("p a f -> p (a f)")).then_inc(loaded[b], 16)
                else:
                    sp.dma_start(flat(rows[0:n_p, b, 0:n_r]), rest).then_inc(loaded[b], 16)

            def store3(group, turn, b):
                n_p, n_r = size(group)
                result = results[b % 2]
                if n_p == P:
                    sp.dma_start(out_full[:, bass.ds(group, 1), :].rearrange("p a f -> p (a f)"), flat(result)).then_inc(out_stored[b % 2], 16)
                else:
                    sp.dma_start(out_rest, flat(result[0:n_p, 0:n_r])).then_inc(out_stored[b % 2], 16)

            def nodes3(group, turn, b):
                sp.wait_ge(summed, group * 2 + 2)
                following = not isinstance(group, int) or group + SLOTS < GROUPS
                if following:
                    load3("x", group + SLOTS, b)
                store3(group, turn, b)
                if following:
                    load3("pre", group + SLOTS, b)
            for group in range(SLOTS):
                load3("x", group, group)
                load3("pre", group, group)
            over_groups3(sp, nodes3)
            for b in range(2):
                sp.wait_ge(out_stored[b], 16 * len(range(b, GROUPS, 2)))

        @block.gpsimd
        def _(pool):
            nc.gpsimd.memset(zeros, 0.0).then_inc(zeros_set, 1)
            pool.wait_ge(zeros_set, 1)
            for k in range(CLEARS_AHEAD):
                pool.dma_start(pre_by_p[:, k * CLEAR * H2:(k + 1) * CLEAR * H2], zeros).then_inc(pre_cleared[k], 16)
            nc.gpsimd.memset(ident[:], 0.0)
            nc.gpsimd.memset(earlier[:], 1.0)
            nc.gpsimd.iota(iota_i[:], pattern=[[P, 2]], base=0, channel_multiplier=1).then_inc(pool_self, 1)
            pool.wait_ge(pool_self, 1)
            nc.gpsimd.affine_select(out=ident[:], in_=ident[:], compare_op=ALU.not_equal, fill=1.0, base=0,
                                    pattern=[[-1, P]], channel_multiplier=1)
            nc.gpsimd.affine_select(out=earlier[:], in_=earlier[:], compare_op=ALU.is_gt, fill=0.0, base=0,
                                    pattern=[[-1, P]], channel_multiplier=1)
            nc.gpsimd.memset(ones[:], 1.0).then_inc(pool_const, 1)

            pool.dma_start(Wmsg[:, IN], W_in.rearrange("(c p) n -> p c n", p=P)).then_inc(weights_in, 16)
            pool.dma_start(Wmsg[:, OUT], W_out.rearrange("(c p) n -> p c n", p=P)).then_inc(weights_in, 16)
            for d in range(2):
                pool.dma_start(Wx[:, d], W_x2i[d * D:(d + 1) * D, :].rearrange("(c p) n -> p c n", p=P)).then_inc(weights_in, 16)
            pool.dma_start(Wh[:], W_h2h.rearrange("(c p) n -> p c n", p=P)).then_inc(weights_in, 16)
            for a, where in ((gamma, gb[:, 0]), (beta, gb[:, 1]), (b_in, bmsg[:, IN]), (b_out, bmsg[:, OUT])):
                for c in range(KC):
                    pool.dma_start(where[:, c:c + 1], a[c * P:(c + 1) * P].rearrange("(p o) -> p o", o=1)).then_inc(weights_in, 16)
            pool.dma_start(bx_row[:], b_x2i.rearrange("(o n) -> o n", o=1)).then_inc(weights_in, 16)

            with pool.Fori(1, CLEARS // CLEARS_AHEAD) as i:
                for k in range(CLEARS_AHEAD):
                    pool.wait_ge(pre_cleared[k], i * 16)
                    pool.dma_start(pre_by_p[:, bass.ds((i * CLEARS_AHEAD + k) * (CLEAR * H2), CLEAR * H2)],
                                   zeros).then_inc(pre_cleared[k], 16)
            for k, (r, n) in enumerate(REST_CLEARS):
                pool.dma_start(pre_by_p[:, r * H2:(r + n) * H2], zeros[:, 0:n * H2]).then_inc(rest_cleared, 16)

            def gather(t, b):
                before(pool, g_ready, t, SLOTS)
                nc.gpsimd.tensor_copy(gidx[:, b, :], gather_cols[:, bass.ds(t, 1), :].rearrange("p a d -> p (a d)")).then_inc(gidx_ready, 1)
                copied = value(pool, t + 1)
                pool.wait_ge(edge_tables, 1)
                pool.wait_ge(gidx_ready, copied)
                for d in range(2):
                    nc.gpsimd.indirect_dma_start(
                        out=xg[d][b][:, :], out_offset=None, in_=x,
                        in_offset=bass.IndirectOffsetOnAxis(ap=gidx[:, b, d:d + 1], axis=0)).then_inc(gathered[b], 16)

            def scatter(t, b):
                pool.wait_ge(rows_u_ready, t + 1)
                pool.wait_ge(pre_in_saved, t + 1)
                pool.wait_ge(pre_out_saved, t + 1)
                if is_first(t):
                    for k in range(CLEARS_AHEAD):
                        pool.wait_ge(pre_cleared[k], 16 * (CLEARS // CLEARS_AHEAD))
                    pool.wait_ge(rest_cleared, 16 * len(REST_CLEARS))
                else:
                    added = value(pool, t * 32)
                    pool.wait_ge(edge_tables, 1)
                    pool.wait_ge(scattered, added)
                for d in range(2):
                    nc.gpsimd.indirect_dma_start(
                        out=pre, out_offset=bass.IndirectOffsetOnAxis(ap=rows_u[d][b][:, 0:1], axis=0),
                        in_=pre_new[d][b][:, :], in_offset=None, compute_op=ALU.add).then_inc(scattered, 16)

            pool.wait_ge(edge_tables, 1)
            for t in range(SLOTS):
                gather(t, t)

            def tile(t, turn, b):
                scatter(t, b)
                if not (isinstance(t, int) and t + SLOTS >= TILES):
                    gather(t + SLOTS, b)
            over_tiles(pool, tile)

            def scale_rows(p):
                pool.wait_ge(h3T_ready, p.index + 1)
                h = hs[0:p.parts, p.slot, p.j0:p.j1, :]
                nc.gpsimd.tensor_tensor(h, h, A_rows[0:p.parts, 0:p.rows, :], ALU.mult).then_inc(bn_scaled, 1)

            def shift_rows(p):
                pool.wait_ge(bn_scaled, p.index + 1)
                h = hs[0:p.parts, p.slot, p.j0:p.j1, :]
                nc.gpsimd.tensor_tensor(h, h, C_rows[0:p.parts, 0:p.rows, :], ALU.add).then_inc(bn_h_ready, 1)

            def finish(p):
                pool.wait_ge(mixed, p.index + 1)
                if p.q == 0:
                    before(pool, out_stored[p.slot % 2], p.turn * 2 + p.slot // 2, 1, 16)
                nc.gpsimd.tensor_tensor(results[p.slot % 2][0:p.parts, p.j0:p.j1, :], hs[0:p.parts, p.slot, p.j0:p.j1, :],
                                        xs[0:p.parts, p.slot, p.j0:p.j1, :], ALU.add).then_inc(summed, 1)

            def pair(p):
                if p.shifted(1).there:
                    scale_rows(p.shifted(1))
                if p.shifted(-3).there:
                    finish(p.shifted(-3))
                if p.shifted(1).there:
                    shift_rows(p.shifted(1))
            scale_rows(Pair(0, 0, 0, 0))
            shift_rows(Pair(0, 0, 0, 0))
            over_pairs(pool, pair)
            for k in (-2, -1, 0):
                finish(LAST.shifted(k))

        @block.scalar
        def _(act):
            act.wait_ge(pads_set, 1)
            act.wait_ge(M_ready, 2 * KC)
            def relu_rows(group, b, j0, j1):
                n_p, _ = size(group)
                for j in range(j0, j1):
                    ins = nc.scalar.activation(hs[0:n_p, b, j, :], xs[0:n_p, b, j, :], ACT.Relu,
                                               bias=ln_b[0:n_p, bass.ds(group, 1), j], scale=ln_r[0:n_p, bass.ds(group, 1), j])
                return ins

            def nodes1(group, turn, b):
                n_p, n_r = size(group)
                act.wait_ge(var_ready, group + 1)
                nc.scalar.activation(ln_std[0:n_p, b, 0:n_r], ln_mv[0:n_p, b, 0:n_r, 1], ACT.Sqrt,
                                     bias=eps_col[0:n_p, :]).then_inc(std_ready, 1)
                if not is_first(group):
                    relu1(group - 1, (b - 1) % SLOTS)

            def relu1(group, b):
                act.wait_ge(ln_ready, group + 1)
                before(act, hT_ready, group, SLOTS)
                relu_rows(group, b, 0, size(group)[1]).then_inc(h_ready, 1)
            over_groups(act, nodes1)
            relu1(GROUPS - 1, (GROUPS - 1) % SLOTS)

            act.wait_ge(bn_var, 1)
            nc.scalar.activation(bn_std[:], bn_mv[:, :, 1], ACT.Sqrt, bias=eps_col[:]).then_inc(bn_std_ready, 1)

            def save_in(t, b):
                act.wait_ge(pre_in_ready, t + 1)
                before(act, scattered, t, SLOTS, 32)
                before(act, pre_out_ready, t, SLOTS)
                nc.scalar.copy(pre_new[IN][b][:, :], pre_ps[IN][b % 2][:, :]).then_inc(pre_in_saved, 1)

            def save_out(t, b):
                act.wait_ge(pre_out_ready, t + 1)
                before(act, scattered, t, SLOTS, 32)
                nc.scalar.copy(pre_new[OUT][b][:, :], pre_ps[OUT][b % 2][:, :]).then_inc(pre_out_saved, 1)

            def tile(t, turn, b):
                act.wait_ge(evar_ready, t + 1)
                nc.scalar.activation(e_std[:, b, :], e_mv[:, b, :, 1], ACT.Sqrt, bias=eps_col[:]).then_inc(estd_ready, 1)
                act.wait_ge(eln_ready, t + 1)
                before(act, gT_ready, t, SLOTS)
                for d in range(2):
                    ins = nc.scalar.activation(g[:, b, d, :], xg[d][b][:, :], ACT.Relu,
                                               bias=e_b[:, b, d:d + 1], scale=e_r[:, b, d:d + 1])
                ins.then_inc(g_ready, 1)
                if not (isinstance(t, int) and t < 2):
                    save_out(t - 2, (b - 2) % SLOTS)
                act.wait_ge(gT_ready, t + 1)
                before(act, projected, t, SLOTS)
                nc.scalar.copy(gT_hi[:, b], gT_ps[b % 2])
                nc.scalar.copy(s_hi[:, b].rearrange("p d r -> p (d r)"), s_ps[b % 2]).then_inc(gT_hi_ready, 1)
                if not is_first(t):
                    save_in(t - 1, (b - 1) % SLOTS)
            over_tiles(act, tile)
            save_out(TILES - 2, (TILES - 2) % SLOTS)
            save_in(TILES - 1, (TILES - 1) % SLOTS)
            save_out(TILES - 1, (TILES - 1) % SLOTS)

            def relu3(p):
                act.wait_ge(x3_in[p.slot], p.turn * 16 + 16)
                before(act, summed, p.index, 2 * SLOTS)
                relu_rows(p.group, p.slot, p.j0, p.j1).then_inc(h3_ready, 1)

            def save_hi(p):
                act.wait_ge(h3T_ready, p.index + 1)
                before(act, own_ready, p.index, 4)
                nc.scalar.copy(hT_hi[:, p.buf, 0:p.rows, :, 0:p.parts], hT_ps3[p.buf][:, 0:p.rows, :, 0:p.parts]).then_inc(h3T_hi, 1)

            def tanh(p):
                act.wait_ge(gates_in, p.index + 1)
                gates = pres[0:p.parts, p.slot, p.j0:p.j1, :]
                nc.scalar.activation(gates, gates, ACT.Tanh).then_inc(gates_ready, 1)

            def pair(p):
                if p.shifted(1).there:
                    save_hi(p.shifted(1))
                if p.shifted(2).there:
                    relu3(p.shifted(2))
                if p.shifted(-1).there:
                    tanh(p.shifted(-1))
            for k in range(2):
                relu3(Pair(0, 0, 0, 0).shifted(k))
            save_hi(Pair(0, 0, 0, 0))
            over_pairs(act, pair)
            tanh(LAST)

        @block.vector
        def _(dve):
            v = nc.vector
            own = [0]

            def link(ins):
                own[0] += 1
                ins.then_inc(dve_self, 1)
                dve.wait_ge(dve_self, own[0])

            v.memset(eps_col[:], EPS).then_inc(pads_set, 1)
            v.memset(edge_rows_i[:], PAD_ROW)
            v.memset(edge_rows[:, 2:4], 0.0).then_inc(pads_set, 1)
            v.memset(ones_r[:].bitcast(F32), 1.0)
            dve.wait_ge(pool_const, 1)
            link(v.tensor_copy(dummy_rows[:], iota_i[:]))
            link(v.tensor_scalar(row_masks[:, 0:1], dummy_rows[:, 0:1], 2.0, None, ALU.is_ge))
            v.tensor_scalar(row_masks[:, 1:2], row_masks[:, 0:1], -1.0, None, ALU.mult)
            link(v.scalar_tensor_tensor(row_masks[:, 2:3], row_masks[:, 0:1], -2.0, dummy_rows[:, 0:1], ALU.mult, ALU.add))
            v.tensor_scalar(row_masks[:, 3:4], row_masks[:, 2:3], -1.0, 1.0, ALU.mult, ALU.add)
            link(v.tensor_scalar(dummy_rows[:], dummy_rows[:], float(DUMMY), None, ALU.add))
            dve.wait_ge(edges_in, 12 * 16)
            v.tensor_copy(edge_rows[:, 0:2], edge_rows_i[:]).then_inc(rows_ready, 1)
            for blk in range(2):
                w = (P, TILES - P)[blk]
                dve.wait_ge(edgeT_ready, blk + 1)
                link(v.tensor_copy(edge_cols[:, blk * P:blk * P + w, :].rearrange("p t k -> p k t"),
                                   bank[blk][:, :].rearrange("p (k t) -> p k t", k=4)[:, :, 0:w]))
            v.tensor_scalar(gather_cols[:, :, 0], edge_cols[:, :, 1], float(N - 1), None, ALU.min)
            v.tensor_scalar(gather_cols[:, :, 1], edge_cols[:, :, 0], float(N - 1), None, ALU.min).then_inc(edge_tables, 1)
            for d in range(2):
                dve.wait_ge(WT_ready, d + 1)
                v.tensor_copy(WmsgT[:, d], bank[2 + d][:, :].rearrange("p (c n) -> p c n", c=KC)).then_inc(WT_saved, 1)
            for d in range(2):
                for c in range(KC):
                    dve.wait_ge(M_ready, d * KC + c + 1)
                    v.tensor_copy(M[:, d, c, :], bank[4 + d * KC + c][:, :]).then_inc(M_saved, 1)

            def columns(group, b):
                n_p, n_r = size(group)
                dve.wait_ge(hT_ready, group + 1)
                for c in range(KC):
                    ins = v.bn_stats(col_stats[:, c, bass.ds(group, 1), :].rearrange("p a s -> p (a s)"), hT_ps1[b][c][:, 0:n_r * n_p])
                ins.then_inc(hT_used, 1)

            def factor(group, b):
                n_p, n_r = size(group)
                dve.wait_ge(std_ready, group + 1)
                v.reciprocal(ln_r[0:n_p, bass.ds(group, 1), 0:n_r].rearrange("p a j -> p (a j)"),
                             ln_std[0:n_p, b, 0:n_r]).then_inc(rstd_ready, 1)

            def offset(group, b):
                n_p, n_r = size(group)
                dve.wait_ge(rstd_ready, group + 1)
                v.scalar_tensor_tensor(ln_b[0:n_p, bass.ds(group, 1), 0:n_r].rearrange("p a j -> p (a j)"), ln_mv[0:n_p, b, 0:n_r, 0], -1.0,
                                       ln_r[0:n_p, bass.ds(group, 1), 0:n_r].rearrange("p a j -> p (a j)"), ALU.mult, ALU.mult).then_inc(ln_ready, 1)

            def nodes1(group, turn, b):
                n_p, n_r = size(group)
                last = (b - 1) % SLOTS
                dve.wait_ge(x_in[b], turn * 16 + 16)
                for j in range(n_r):
                    ins = v.bn_stats(ln_stats[0:n_p, b, j, :], xs[0:n_p, b, j, :])
                ins.then_inc(stats_ready, 1)
                if not is_first(group):
                    factor(group - 1, last)
                done = value(dve, group + 1)
                dve.wait_ge(pool_const, 1)
                dve.wait_ge(stats_ready, done)
                for j in range(n_r):
                    ins = v.bn_aggr(ln_mv[0:n_p, b, j, :], ln_stats[0:n_p, b, j, :])
                ins.then_inc(var_ready, 1)
                if not is_first(group):
                    offset(group - 1, last)
                if not (isinstance(group, int) and group < 3):
                    columns(group - 3, (b - 3) % SLOTS)
            over_groups(dve, nodes1)
            factor(GROUPS - 1, (GROUPS - 1) % SLOTS)
            offset(GROUPS - 1, (GROUPS - 1) % SLOTS)
            for group in range(GROUPS - 3, GROUPS):
                columns(group, group % SLOTS)
            dve.wait_ge(hT_used, GROUPS)

            for c in range(KC):
                ins = v.bn_aggr(bn_mv[:, c, :], col_stats[:, c].rearrange("p g s -> p (g s)"))
            ins.then_inc(bn_var, 1)
            dve.wait_ge(weights_in, 14 * 16)
            dve.wait_ge(bn_std_ready, 1)
            link(v.reciprocal(bn_rstd[:], bn_std[:]))
            link(v.tensor_tensor(bn_A[:], gb[:, 0], bn_rstd[:], ALU.mult))
            link(v.tensor_tensor(bn_t[:], bn_mv[:, :, 0], bn_A[:], ALU.mult))
            link(v.tensor_tensor(bn_C[:], gb[:, 1], bn_t[:], ALU.subtract))
            for c in range(KC):
                for k, col in enumerate((bn_C[:, c:c + 1], bmsg[:, IN, c:c + 1], bmsg[:, OUT, c:c + 1])):
                    v.tensor_scalar(col4[:, k, c, :], ones[:, 0:4], col, None, ALU.mult)
                v.tensor_scalar(rep[:, 0, c, :], ones[:], bn_A[:, c:c + 1], None, ALU.mult)
                ins = v.tensor_scalar(rep[:, 1, c, :], ones[:], bn_C[:, c:c + 1], None, ALU.mult)
            ins.then_inc(bn_cols_ready, 1)

            def halved(to, frm, scale):
                v.tensor_scalar(to[:, 0:D], frm[:, 0:D], scale, 0.5, ALU.mult, ALU.mult)
                link(v.tensor_scalar(to[:, D:H2], frm[:, D:H2], scale, None, ALU.mult))

            for c in range(KC):
                for raw, hi, lo in ((M[:, IN, c], M_hi[:, IN, c], M_lo[:, IN, c]), (M[:, OUT, c], M_hi[:, OUT, c], M_lo[:, OUT, c]),
                                    (Wh[:, c], Wh_hi[:, c], Wh_lo[:, c])):
                    halved(scaled, raw, bn_A[:, c:c + 1])
                    link(v.tensor_copy(hi, scaled))
                    link(v.tensor_tensor(lo, scaled, hi.bitcast(F32), ALU.subtract))
            for k in range(3):
                dve.wait_ge(vec_ready, k + 1)
                halved(vec4, bank[k][0:4, :], 1.0)
                link(v.tensor_copy(vec4_hi[:], vec4))
                link(v.tensor_tensor(vec4_lo, vec4, vec4_hi[:].bitcast(F32), ALU.subtract))
                link(v.tensor_scalar(vec4, vec4_hi[:].bitcast(F32), row_masks[0:4, 3:4], None, ALU.mult))
                link(v.scalar_tensor_tensor(const4[:, k, :], vec4_lo, row_masks[0:4, 2:3], vec4, ALU.mult, ALU.add))
            dve.wait_ge(rows_T, 1)
            for j in range(2):
                v.tensor_copy(A_rows[:, j, :], bank[3][:, 0:D])
                ins = v.tensor_copy(C_rows[:, j, :], bank[3][:, D:2 * D])
            ins.then_inc(weights_ready, 1)

            def stage(t, b):
                v.tensor_copy(cols[:, b, :], edge_cols[:, bass.ds(t, 1), :].rearrange("p a k -> p (a k)")).then_inc(cols_ready, 1)

            def save_lo(t, b):
                dve.wait_ge(gT_hi_ready, t + 1)
                v.tensor_tensor(gT_lo[:, b], gT_ps[b % 2], gT_hi[:, b].bitcast(F32), ALU.subtract)
                v.scalar_tensor_tensor(s4[:, b].rearrange("p d r -> p (d r)"), s_hi[:, b].bitcast(F32).rearrange("p d r -> p (d r)"), row_masks[0:4, 1:2],
                                       s_ps[b % 2], ALU.mult, ALU.add).then_inc(gT_lo_ready, 1)

            def tile(t, turn, b):
                s = b % 2
                if not (isinstance(t, int) and t + 1 >= TILES):
                    stage(t + 1, (b + 1) % SLOTS)
                dve.wait_ge(gathered[b], turn * 32 + 32)
                for d in range(2):
                    ins = v.bn_stats(e_stats[:, b, d, :], xg[d][b][:, :])
                ins.then_inc(estats_ready, 1)
                done = value(dve, t + 1)
                dve.wait_ge(pool_const, 1)
                dve.wait_ge(estats_ready, done)
                for d in range(2):
                    ins = v.bn_aggr(e_mv[:, b, d, :], e_stats[:, b, d, :])
                ins.then_inc(evar_ready, 1)
                dve.wait_ge(cols_ready, t + 1)
                dve.wait_ge(idxT_ready, t + 1)
                v.tensor_tensor(shift[:, b, :], dummy_rows[:], cols[:, b, 0:2], ALU.subtract)
                for d in range(2):
                    ins = v.scalar_tensor_tensor(junk[:, d, :], idx_ps[s][:, d, :], cols[:, b, d:d + 1], earlier[:],
                                                 ALU.is_equal, ALU.mult, accum_out=dups[:, b, d:d + 1])
                ins.then_inc(dups_ready, 1)
                before(dve, gT_ready, t, SLOTS)
                for d in range(2):
                    ins = v.tensor_scalar(merge[:, b, d, :], idx_ps[s][:, d, :], cols[:, b, d:d + 1], cols[:, b, 2 + d:3 + d],
                                          ALU.is_equal, ALU.mult)
                    if d == 0:
                        dve.wait_ge(dups_ready, t + 1)
                        v.scalar_tensor_tensor(kept[:, b, :], dups[:, b, :], 0.0, shift[:, b, :], ALU.is_gt, ALU.mult).then_inc(kept_ready, 1)
                ins.then_inc(merge_ready, 1)
                dve.wait_ge(kept_ready, t + 1)
                v.tensor_tensor(rows_f[:, b, :], kept[:, b, :], cols[:, b, 0:2], ALU.add).then_inc(rows_ready2, 1)
                before(dve, pre_out_ready, t, SLOTS)
                dve.wait_ge(rows_ready2, t + 1)
                v.tensor_tensor(moved[:, b, :], dummy_rows[:, 0:1], rows_f[:, b, 0:1], ALU.subtract)
                v.scalar_tensor_tensor(cross[:, b, :], idx_ps[s][:, OUT, :], rows_f[:, b, IN:IN + 1], ones[:],
                                       ALU.is_equal, ALU.mult, accum_out=taken[:, b, :]).then_inc(cross_ready, 1)
                dve.wait_ge(estd_ready, t + 1)
                v.reciprocal(e_r[:, b, :], e_std[:, b, :]).then_inc(erstd_ready, 1)
                dve.wait_ge(cross_ready, t + 1)
                v.scalar_tensor_tensor(moved2[:, b, :], taken[:, b, :], 0.0, moved[:, b, :], ALU.is_gt, ALU.mult).then_inc(moved2_ready, 1)
                dve.wait_ge(erstd_ready, t + 1)
                v.scalar_tensor_tensor(e_b[:, b, :], e_mv[:, b, :, 0], -1.0, e_r[:, b, :], ALU.mult, ALU.mult).then_inc(eln_ready, 1)
                before(dve, scattered, t, SLOTS, 32)
                v.tensor_copy(rows_u[OUT][b][:], rows_f[:, b, OUT:OUT + 1])
                dve.wait_ge(moved2_ready, t + 1)
                v.tensor_tensor(rows_u[IN][b][:], moved2[:, b, :], rows_f[:, b, IN:IN + 1], ALU.add).then_inc(rows_u_ready, 1)
                if not is_first(t):
                    save_lo(t - 1, (b - 1) % SLOTS)
            stage(0, 0)
            over_tiles(dve, tile)
            save_lo(TILES - 1, (TILES - 1) % SLOTS)

            def save_lo3(p):
                dve.wait_ge(h3T_hi, p.index + 1)
                v.tensor_tensor(hT_lo[:, p.buf, 0:p.rows, :, 0:p.parts], hT_ps3[p.buf][:, 0:p.rows, :, 0:p.parts],
                                hT_hi[:, p.buf, 0:p.rows, :, 0:p.parts].bitcast(F32), ALU.subtract).then_inc(h3T_lo, 1)

            def add_own(p, j):
                sums = pres[0:p.parts, p.slot, j, :]
                return v.tensor_tensor(sums, sums, node_ps[j][0:p.parts, :], ALU.add)

            def operands(p):
                rows = pres[0:p.parts, p.slot, p.j0:p.j1, :]
                return hs[0:p.parts, p.slot, p.j0:p.j1, :], rows[:, :, 0:D], rows[:, :, D:H2]

            def mix_a(p):
                h, _, new = operands(p)
                dve.wait_ge(gates_ready, p.index + 1)
                dve.wait_ge(bn_h_ready, p.index + 1)
                v.tensor_tensor(h, h, new, ALU.subtract).then_inc(diff_ready, 1)

            def mix_b(p):
                h, gate, _ = operands(p)
                dve.wait_ge(diff_ready, p.index + 1)
                v.scalar_tensor_tensor(h, gate, 1.0, h, ALU.add, ALU.mult).then_inc(gated_ready, 1)

            def mix_c(p):
                h, _, new = operands(p)
                dve.wait_ge(gated_ready, p.index + 1)
                v.scalar_tensor_tensor(h, h, 0.5, new, ALU.mult, ALU.add).then_inc(mixed, 1)

            def steps(splitting, adding, mixing):
                if adding:
                    if adding.q == 0:
                        dve.wait_ge(pre_in[adding.slot], adding.turn * 16 + 16)
                    dve.wait_ge(own_ready, adding.index + 1)
                    ins = add_own(adding, adding.j0)
                    if adding.rows == 1:
                        ins.then_inc(gates_in, 1)
                if mixing:
                    mix_a(mixing)
                if adding and adding.rows == 2:
                    add_own(adding, adding.j0 + 1).then_inc(gates_in, 1)
                if mixing:
                    mix_b(mixing)
                if splitting:
                    save_lo3(splitting)
                if mixing:
                    mix_c(mixing)

            def pair(p):
                steps(*(p.shifted(k) if p.shifted(k).there else None for k in (1, -1, -2)))
            save_lo3(Pair(0, 0, 0, 0))
            over_pairs(dve, pair)
            steps(None, LAST, LAST.shifted(-1))
            steps(None, None, LAST)

        @block.tensor
        def _(pe):
            mm, transpose = nc.tensor.matmul, nc.tensor.transpose
            pe.wait_ge(pool_const, 1)
            pe.wait_ge(rows_ready, 1)
            for blk in range(2):
                w = (P, TILES - P)[blk]
                for k in range(4):
                    ins = transpose(bank[blk][:, k * P:k * P + w], edge_rows[0:w, k, blk, :], ident[0:w, 0:w])
                ins.then_inc(edgeT_ready, 1)
            pe.wait_ge(weights_in, 14 * 16)
            for d in range(2):
                for c2 in range(KC):
                    for c1 in range(KC):
                        ins = transpose(bank[2 + d][:, c2 * D + c1 * P:c2 * D + (c1 + 1) * P],
                                        Wmsg[:, d, c1, c2 * P:(c2 + 1) * P], ident[:])
                ins.then_inc(WT_ready, 1)
            for d in range(2):
                pe.wait_ge(WT_saved, d + 1)
                for c1 in range(KC):
                    for c2 in range(KC):
                        ins = mm(bank[4 + d * KC + c1][:, :], WmsgT[:, d, c2, c1 * P:(c1 + 1) * P], Wx[:, d, c2, :],
                                 start=(c2 == 0), stop=(c2 == KC - 1))
                    ins.then_inc(M_ready, 1)

            pe.wait_ge(edge_tables, 1)
            pe.wait_ge(M_saved, 2 * KC)

            def nodes1(group, turn, b):
                n_p, n_r = size(group)
                pe.wait_ge(h_ready, group + 1)
                before(pe, hT_used, group, SLOTS)
                for c in range(KC):
                    for j in range(n_r):
                        ins = transpose(hT_ps1[b][c][:, j * n_p:(j + 1) * n_p], hs[0:n_p, b, j, c * P:(c + 1) * P],
                                        ident[0:n_p, 0:n_p])
                ins.then_inc(hT_ready, 1)
            over_groups(pe, nodes1)

            pe.wait_ge(bn_cols_ready, 1)
            for d in range(2):
                for c in range(KC):
                    mm(bank[d][0:4, :], col4[:, 0, c, :], M[:, d, c, :], start=(c == 0), stop=False)
                for c in range(KC):
                    ins = mm(bank[d][0:4, :], col4[:, 1 + d, c, :], Wx[:, d, c, :], start=False, stop=(c == KC - 1))
                ins.then_inc(vec_ready, 1)
            for c in range(KC):
                mm(bank[2][0:4, :], col4[:, 0, c, :], Wh[:, c, :], start=(c == 0), stop=False)
            mm(bank[2][0:4, :], ones[0:1, 0:4], bx_row[:], start=False, stop=True).then_inc(vec_ready, 1)
            for k in range(2):
                for c in range(KC):
                    ins = transpose(bank[3][:, k * D + c * P:k * D + (c + 1) * P], rep[:, k, c, :], ident[:])
            ins.then_inc(rows_T, 1)
            pe.wait_ge(weights_ready, 1)

            def exact3(to, left_hi, left_lo, right_hi, right_lo, first, last):
                mm(to, left_hi, right_hi, start=first, stop=False)
                mm(to, left_hi, right_lo, start=False, stop=False)
                return mm(to, left_lo, right_hi, start=False, stop=last)

            def spread_indices(t, b):
                pe.wait_ge(cols_ready, t + 1)
                before(pe, gT_lo_ready, t, 2)
                for d in range(2):
                    ins = transpose(idx_ps[b % 2][:, d, :], cols[:, b, d:d + 1].to_broadcast([P, P]), ident[:])
                ins.then_inc(idxT_ready, 1)

            def merge_rows(t, b):
                pe.wait_ge(g_ready, t + 1)
                pe.wait_ge(merge_ready, t + 1)
                before(pe, gT_lo_ready, t, 2)
                for d in range(2):
                    for c in range(KC):
                        mm(gT_ps[b % 2][:, d, c, :], g[:, b, d, c * P:(c + 1) * P], merge[:, b, d, :], start=True, stop=True)
                pe.wait_ge(cross_ready, t + 1)
                mm(s_ps[b % 2], ones[:, 0:4], merge[:, b].rearrange("p d r -> p (d r)"),
                   start=True, stop=True).then_inc(gT_ready, 1)

            def project(t, b):
                pe.wait_ge(gT_lo_ready, t + 1)
                for d, saved in ((IN, pre_in_saved), (OUT, pre_out_saved)):
                    before(pe, saved, t, 2)
                    to = pre_ps[d][b % 2][:, :]
                    for c in range(KC):
                        exact3(to, gT_hi[:, b, d, c, :], gT_lo[:, b, d, c, :], M_hi[:, d, c, :], M_lo[:, d, c, :], c == 0, False)
                    ins = mm(to, s4[:, b, d, :], const4[:, d, :], start=False, stop=(d == IN))
                    ins.then_inc(pre_in_ready if d == IN else projected, 1)

            def add_cross(t, b):
                pe.wait_ge(pre_in_saved, t + 1)
                pe.wait_ge(cross_ready, t + 1)
                mm(pre_ps[OUT][b % 2][:, :], cross[:, b, :], pre_new[IN][b][:, :], start=False, stop=True).then_inc(pre_out_ready, 1)

            def tile(t, turn, b):
                if not (isinstance(t, int) and t < 2):
                    add_cross(t - 2, (b - 2) % SLOTS)
                merge_rows(t, b)
                if not (isinstance(t, int) and t + 1 >= TILES):
                    spread_indices(t + 1, (b + 1) % SLOTS)
                if not is_first(t):
                    project(t - 1, (b - 1) % SLOTS)
            spread_indices(0, 0)
            over_tiles(pe, tile)
            add_cross(TILES - 2, (TILES - 2) % SLOTS)
            project(TILES - 1, (TILES - 1) % SLOTS)
            add_cross(TILES - 1, (TILES - 1) % SLOTS)

            pe.wait_ge(gT_lo_ready, TILES)
            pe.wait_ge(pre_out_saved, TILES)

            def transpose_pair(p):
                pe.wait_ge(h3_ready, p.index + 1)
                before(pe, h3T_lo, p.index, 4)
                for j in range(p.j0, p.j1):
                    for c in range(KC):
                        ins = transpose(hT_ps3[p.buf][:, j - p.j0, c, 0:p.parts], hs[0:p.parts, p.slot, j, c * P:(c + 1) * P],
                                        ident[0:p.parts, 0:p.parts])
                ins.then_inc(h3T_ready, 1)

            def own_product(p):
                pe.wait_ge(h3T_lo, p.index + 1)
                before(pe, gates_in, p.index, 2)
                for j in range(p.j0, p.j1):
                    to = node_ps[j][0:p.parts, :]
                    mm(to, ones_r[0:2, 0:p.parts], const4[0:2, 2, :], start=True, stop=False)
                    for c in range(KC):
                        ins = exact3(to, hT_hi[:, p.buf, j - p.j0, c, 0:p.parts], hT_lo[:, p.buf, j - p.j0, c, 0:p.parts],
                                     Wh_hi[:, c, :], Wh_lo[:, c, :], False, c == KC - 1)
                ins.then_inc(own_ready, 1)

            def pair(p):
                if p.shifted(1).there:
                    transpose_pair(p.shifted(1))
                own_product(p)
            for k in range(1):
                transpose_pair(Pair(0, 0, 0, 0).shifted(k))
            over_pairs(pe, pair)


INPUTS = ["x", "src", "dst", "edge_weight", "edge_weight_n2", "L0_gnn_gamma", "L0_gnn_beta", "L0_gnn_W_in", "L0_gnn_b_in",
          "L0_gnn_W_out", "L0_gnn_b_out", "L0_gnn_W_x2i", "L0_gnn_b_x2i", "L0_gnn_W_h2h"]


def kernel(**inputs):
    import concourse.bacc as bacc
    from concourse.bass_utils import run_bass_kernel_spmd

    nc = bacc.Bacc("TRN2", target_bir_lowering=False, num_devices=1)
    arrays, aps = {}, []
    for name in INPUTS:
        a = np.ascontiguousarray(inputs[name])
        arrays[f"in_{name}"] = a
        aps.append(nc.dram_tensor(f"in_{name}", a.shape, mybir.dt.from_np(a.dtype), kind="ExternalInput").ap())
    x = inputs["x"]
    out = nc.dram_tensor("out", x.shape, F32, kind="ExternalOutput").ap()
    build(nc, *aps, out)
    r = run_bass_kernel_spmd(nc, [arrays], core_ids=[0])
    return r.results[0]["out"]
```

```python
from contextlib import ExitStack

import concourse.bass as bass
from concourse import mybir
import numpy as np

F32 = mybir.dt.float32
F32R = mybir.dt.float32r
I32 = mybir.dt.int32
U32 = mybir.dt.uint32
ALU = mybir.AluOpType
ACT = mybir.ActivationFunctionType

P = 128
EPS = 1e-5
SLOTS = 4
IN, OUT = 0, 1


def value(engine, n):
    return n if isinstance(n, int) else engine.to_reg(n)


def before(engine, sem, step, lag, per=1):
    if not (isinstance(step, int) and step < lag):
        engine.wait_ge(sem, (step - lag + 1) * per)


def build(nc, x, src, dst, w_in_edge, w_out_edge, gamma, beta, W_in, b_in, W_out, b_out, W_x2i, b_x2i, W_h2h, out):
    N, D = x.shape
    E = src.shape[0]
    H2 = W_h2h.shape[1]
    KC = D // P
    ROWS = 4
    GROUP = P * ROWS
    FULL = N // GROUP
    REST = N - FULL * GROUP
    REST_ROWS = -(-REST // P)
    REST_P = REST // REST_ROWS
    GROUPS = FULL + 1
    BODIES = FULL // SLOTS
    assert 0 < REST and REST % (16 * REST_ROWS) == 0 and FULL - BODIES * SLOTS == 1 and KC == 2 and H2 == 2 * D
    TILES = -(-E // P)
    LAST_E = E - (TILES - 1) * P
    assert TILES % SLOTS == 0 and P < TILES <= 2 * P and 0 < LAST_E < P
    DUMMY = N
    PAD_ROW = N + 2 * P
    PRE_PER_P = -(-(PAD_ROW + 1) // P)
    PRE_ROWS = PRE_PER_P * P
    CLEARS = 4 * BODIES
    CLEAR = PRE_PER_P // CLEARS
    CLEARS_AHEAD = 2
    REST_CLEARS = [(r, min(CLEAR, PRE_PER_P - r)) for r in range(CLEARS * CLEAR, PRE_PER_P, CLEAR)]
    assert CLEARS % CLEARS_AHEAD == 0

    pre = nc.dram_tensor("pre_gates", [PRE_ROWS, H2], F32).ap()
    pre_by_p = pre.rearrange("(p r) f -> p (r f)", p=P)

    x_full = x[0:FULL * GROUP, :].rearrange("(g p r) f -> p g (r f)", p=P, r=ROWS)
    x_rest = x[FULL * GROUP:N, :].rearrange("(p r) f -> p (r f)", r=REST_ROWS)
    out_full = out[0:FULL * GROUP, :].rearrange("(g p r) f -> p g (r f)", p=P, r=ROWS)
    out_rest = out[FULL * GROUP:N, :].rearrange("(p r) f -> p (r f)", r=REST_ROWS)
    pre_full = pre[0:FULL * GROUP, :].rearrange("(g p r) f -> p g (r f)", p=P, r=ROWS)
    pre_rest = pre[FULL * GROUP:N, :].rearrange("(p r) f -> p (r f)", r=REST_ROWS)

    ctx = ExitStack()
    with ctx:
        def sb(name, shape, dt=F32):
            return ctx.enter_context(nc.sbuf_tensor(name, shape, dt))

        def sem(name):
            return ctx.enter_context(nc.semaphore(name))

        ident = sb("ident", [P, P])
        earlier = sb("earlier", [P, P])
        ones = sb("ones", [P, P])
        ones_r = sb("ones_r", [2, P], F32R)
        dummy_rows = sb("dummy_rows", [P, 2])
        iota_i = sb("iota_i", [P, 2], I32)
        eps_col = sb("eps_col", [P, 1])
        row_masks = sb("row_masks", [P, 4])
        edge_rows_i = sb("edge_rows_i", [P, 2, 2, P], I32)
        edge_rows = sb("edge_rows", [P, 4, 2, P])
        edge_cols = sb("edge_cols", [P, TILES, 4])
        gather_cols = sb("gather_cols", [P, TILES, 2], U32)
        Wx = sb("Wx", [P, 2, KC, H2])
        Wh = sb("Wh", [P, KC, H2])
        bmsg = sb("bmsg", [P, 2, KC])
        bx_row = sb("bx_row", [1, H2])
        gb = sb("gb", [P, 2, KC])
        M = sb("M", [P, 2, KC, H2])
        M_hi = sb("M_hi", [P, 2, KC, H2], F32R)
        M_lo = sb("M_lo", [P, 2, KC, H2], F32R)
        Wh_hi = sb("Wh_hi", [P, KC, H2], F32R)
        Wh_lo = sb("Wh_lo", [P, KC, H2], F32R)
        col4 = sb("col4", [P, 3, KC, 4])
        const4 = sb("const4", [4, 3, H2], F32R)
        bn_mv = sb("bn_mv", [P, KC, 2])
        bn_std = sb("bn_std", [P, KC])
        bn_rstd = sb("bn_rstd", [P, KC])
        bn_t = sb("bn_t", [P, KC])
        bn_A = sb("bn_A", [P, KC])
        bn_C = sb("bn_C", [P, KC])
        rep = sb("rep", [P, 2, KC, P])
        A_rows = sb("A_rows", [P, 2, D])
        C_rows = sb("C_rows", [P, 2, D])
        xs = sb("xs", [P, SLOTS, ROWS, D])
        hs = sb("hs", [P, SLOTS, ROWS, D])
        Wmsg = hs[:, 0].rearrange("p (d c) n -> p d c n", d=2)
        WmsgT = hs[:, 1].rearrange("p (d c) n -> p d c n", d=2)
        spare = [xs[:, k // 2].rearrange("p r f -> p (r f)")[:, (k % 2) * H2:(k % 2 + 1) * H2] for k in range(2 * SLOTS)]
        scaled, spare4 = spare[0:6], spare[6][0:4, :]
        vec4 = [spare[k][0:4, :] for k in range(3)]
        ln_stats = sb("ln_stats", [P, SLOTS, ROWS, 6])
        ln_mv = sb("ln_mv", [P, SLOTS, ROWS, 2])
        ln_std = sb("ln_std", [P, SLOTS, ROWS])
        ln_r = sb("ln_r", [P, GROUPS, ROWS])
        ln_b = sb("ln_b", [P, GROUPS, ROWS])
        col_stats = sb("col_stats", [P, KC, GROUPS, 6])
        gidx = sb("gidx", [P, SLOTS, 2], U32)
        g = sb("g", [P, SLOTS, 2, D])
        e_stats = sb("e_stats", [P, SLOTS, 2, 6])
        e_mv = sb("e_mv", [P, SLOTS, 2, 2])
        e_std = sb("e_std", [P, SLOTS, 2])
        e_r = sb("e_r", [P, SLOTS, 2])
        e_b = sb("e_b", [P, SLOTS, 2])
        cols = sb("cols", [P, SLOTS, 4])
        merge = sb("merge", [P, SLOTS, 2, P])
        in_hi = sb("in_hi", [P, 2, H2], F32R)
        in_lo = sb("in_lo", [P, 2, H2], F32R)
        cross = sb("cross", [P, SLOTS, P], F32R)
        junk = sb("junk", [P, 2, P])
        dups = sb("dups", [P, SLOTS, 2])
        shift = sb("shift", [P, SLOTS, 2])
        kept = sb("kept", [P, SLOTS, 2])
        rows_f = sb("rows_f", [P, SLOTS, 2])
        to_dummy = sb("to_dummy", [P, SLOTS, 1])
        moved = sb("moved", [P, SLOTS, 1])
        taken = sb("taken", [P, SLOTS, 1])
        rows_u = [[sb(f"rows_u_{d}_{b}", [P, 1], U32) for b in range(SLOTS)] for d in range(2)]
        gT_hi = sb("gT_hi", [P, SLOTS, 2, KC, P], F32R)
        gT_lo = sb("gT_lo", [P, SLOTS, 2, KC, P], F32R)
        s_hi = sb("s_hi", [4, SLOTS, 2, P], F32R)
        s4 = sb("s4", [4, SLOTS, 2, P], F32R)
        pres = sb("pres", [P, SLOTS, ROWS, H2])
        pres_flat = pres[:, :, :, :].rearrange("p b r f -> p (b r f)")
        zeros = pres_flat[:, 0:CLEAR * H2]
        NEW = pres_flat.shape[1] - 2 * SLOTS * H2
        GATHERED = NEW - 2 * SLOTS * D
        assert CLEAR * H2 <= GATHERED
        xg = [[pres_flat[:, GATHERED + (d * SLOTS + b) * D:GATHERED + (d * SLOTS + b + 1) * D] for b in range(SLOTS)] for d in range(2)]
        pre_new = [[pres_flat[:, NEW + (d * SLOTS + b) * H2:NEW + (d * SLOTS + b + 1) * H2] for b in range(SLOTS)] for d in range(2)]
        results = [g[:, 2 * k:2 * k + 2].rearrange("p b d f -> p (b d) f") for k in range(2)]
        hT_hi, hT_lo = gT_hi, gT_lo

        bank = [ctx.enter_context(nc.psum_tensor(f"bank{i}", [P, 512], F32)) for i in range(8)]
        weights = [w for c in range(KC) for w in (M[:, IN, c], M[:, OUT, c], Wh[:, c])]
        weight_parts = [w for c in range(KC) for w in ((M_hi[:, IN, c], M_lo[:, IN, c]), (M_hi[:, OUT, c], M_lo[:, OUT, c]),
                                                       (Wh_hi[:, c], Wh_lo[:, c]))]
        hT_ps1 = [[bank[2 * s + c] for c in range(KC)] for s in range(SLOTS)]
        vec_ps, rows_ps = (bank[4], bank[6], bank[7]), bank[5]
        idx_ps = [bank[s][:, 0:2 * P].rearrange("p (d r) -> p d r", d=2) for s in range(2)]
        s_ps = [bank[s][0:4, 2 * P:4 * P] for s in range(2)]
        gT_ps = [bank[2 + s][:, :].rearrange("p (d c r) -> p d c r", d=2, c=KC) for s in range(2)]
        pre_ps = [[bank[4 + 2 * d + s] for s in range(2)] for d in range(2)]
        hT_ps3 = [bank[s][:, :].rearrange("p (j c r) -> p j c r", j=2, c=KC) for s in range(4)]
        node_ps = [bank[4 + j] for j in range(4)]

        def sems(names):
            return [sem(name) for name in names.split()]

        pool_const, pool_self, pads_set, edges_in, weights_in = sems("pool_const pool_self pads_set edges_in weights_in")
        dve_self, rows_ready, edgeT_ready, edge_tables = sems("dve_self rows_ready edgeT_ready edge_tables")
        WT_ready, WT_saved, M_ready, M_saved = sems("WT_ready WT_saved M_ready M_saved")
        x_in = [sem(f"x_in_{b}") for b in range(SLOTS)]
        zeros_set = sem("zeros_set")
        rest_cleared = sem("rest_cleared")
        pre_cleared = [sem(f"pre_cleared_{k}") for k in range(CLEARS_AHEAD)]
        stats_ready, var_ready, std_ready, rstd_ready, ln_ready = sems("stats_ready var_ready std_ready rstd_ready ln_ready")
        h_ready, hT_ready, hT_used = sems("h_ready hT_ready hT_used")
        bn_var, bn_std_ready, bn_cols_ready, vec_ready, rows_T, rows_saved = sems(
            "bn_var bn_std_ready bn_cols_ready vec_ready rows_T rows_saved")
        scaled_ready, weight_hi_ready, weight_lo_ready, halved_ready, vec_saved, spare_used = sems(
            "scaled_ready weight_hi_ready weight_lo_ready halved_ready vec_saved spare_used")
        gathered = [sem(f"gathered_{b}") for b in range(SLOTS)]
        gidx_ready, cols_ready, idxT_ready = sems("gidx_ready cols_ready idxT_ready")
        estats_ready, evar_ready, estd_ready, erstd_ready, eln_ready, g_ready = sems(
            "estats_ready evar_ready estd_ready erstd_ready eln_ready g_ready")
        merge_ready, dups_ready, kept_ready, rows_f_ready, cross_ready, to_dummy_ready, moved_ready, rows_u_ready = sems(
            "merge_ready dups_ready kept_ready rows_f_ready cross_ready to_dummy_ready moved_ready rows_u_ready")
        gT_ready, gT_hi_ready, gT_lo_ready = sems("gT_ready gT_hi_ready gT_lo_ready")
        in_hi_ready, in_lo_ready = sems("in_hi_ready in_lo_ready")
        pre_in_ready, pre_in_saved, projected, pre_out_ready, pre_out_saved, scattered = sems(
            "pre_in_ready pre_in_saved projected pre_out_ready pre_out_saved scattered")
        x3_in = [sem(f"x3_in_{b}") for b in range(SLOTS)]
        pre_in = [sem(f"pre_in_{b}") for b in range(SLOTS)]
        out_stored = [sem(f"out_stored_{b}") for b in range(2)]
        h3_ready, h3T_ready, h3T_hi, h3T_lo, own_ready, gates_in, gates_ready = sems(
            "h3_ready h3T_ready h3T_hi h3T_lo own_ready gates_in gates_ready")
        bn_scaled, bn_h_ready, diff_ready, gated_ready, mixed, summed = sems(
            "bn_scaled bn_h_ready diff_ready gated_ready mixed summed")

        block = ctx.enter_context(nc.Block())

        def size(group):
            return (REST_P, REST_ROWS) if isinstance(group, int) and group == GROUPS - 1 else (P, ROWS)

        def over_groups(engine, step):
            for b in range(SLOTS):
                step(b, 0, b)
            with engine.Fori(1, BODIES) as i:
                for b in range(SLOTS):
                    step(i * SLOTS + b, i, b)
            for group in range(BODIES * SLOTS, GROUPS):
                step(group, BODIES, group % SLOTS)

        def over_groups3(engine, step):
            for b in range(SLOTS):
                step(b, 0, b)
            with engine.Fori(1, BODIES - 1) as i:
                for b in range(SLOTS):
                    step(i * SLOTS + b, i, b)
            for group in range((BODIES - 1) * SLOTS, GROUPS):
                step(group, group // SLOTS, group % SLOTS)

        def over_tiles(engine, step, tail=1):
            for t in range(2 * SLOTS):
                step(t, t // SLOTS, t % SLOTS)
            with engine.Fori(2, TILES // SLOTS - tail) as i:
                for b in range(SLOTS):
                    step(i * SLOTS + b, i, b)
            for t in range(TILES - tail * SLOTS, TILES):
                step(t, t // SLOTS, t % SLOTS)

        def over_pairs(engine, step):
            for group in range(SLOTS):
                for q in range(2):
                    step(Pair(group, 0, group, q))
            with engine.Fori(1, BODIES - 1) as i:
                for b in range(SLOTS):
                    for q in range(2):
                        step(Pair(i * SLOTS + b, i, b, q))
            for group in range((BODIES - 1) * SLOTS, GROUPS):
                for q in range(2):
                    step(Pair(group, group // SLOTS, group % SLOTS, q))

        class Pair:

            def __init__(self, group, turn, slot, q):
                self.group, self.turn, self.slot, self.q = group, turn, slot, q
                self.parts, rows = size(group)
                self.j0, self.j1 = 2 * q, min(2 * q + 2, rows)
                self.rows = self.j1 - self.j0
                self.index = group * 2 + q
                self.buf = (2 * slot + q) % 4
                self.there = not isinstance(group, int) or 0 <= group < GROUPS

            def shifted(self, k):
                groups, q = divmod(self.q + k, 2)
                turns, slot = divmod(self.slot + groups, SLOTS)
                return Pair(self.group + groups, self.turn + turns, slot, q)

        LAST = Pair(GROUPS - 1, (GROUPS - 1) // SLOTS, (GROUPS - 1) % SLOTS, 1)

        def is_first(step):
            return isinstance(step, int) and step == 0

        def flat(ap):
            return ap.rearrange("p r f -> p (r f)")

        @block.sync
        def _(sp):
            sp.wait_ge(pads_set, 2)
            tail = TILES - 1 - P
            for a, rows in ((dst, edge_rows_i[:, 0]), (src, edge_rows_i[:, 1]),
                            (w_in_edge, edge_rows[:, 2]), (w_out_edge, edge_rows[:, 3])):
                sp.dma_start(rows[:, 0, :], a[0:P * P].rearrange("(t e) -> t e", e=P)).then_inc(edges_in, 16)
                sp.dma_start(rows[0:tail, 1, :],
                             a[P * P:(TILES - 1) * P].rearrange("(t e) -> t e", e=P)).then_inc(edges_in, 16)
                sp.dma_start(rows[tail:tail + 1, 1, 0:LAST_E],
                             a[(TILES - 1) * P:E].rearrange("(t e) -> t e", t=1)).then_inc(edges_in, 16)

            def load1(group, turn, b):
                before(sp, h_ready, group, SLOTS)
                n_p, n_r = size(group)
                if n_p == P:
                    sp.dma_start(flat(xs[:, b]), x_full[:, bass.ds(group, 1), :].rearrange("p a f -> p (a f)")).then_inc(x_in[b], 16)
                else:
                    sp.dma_start(flat(xs[0:n_p, b, 0:n_r]), x_rest).then_inc(x_in[b], 16)

            over_groups(sp, load1)

            sp.wait_ge(h_ready, GROUPS)
            sp.wait_ge(spare_used, 1)

            def load3(what, group, b):
                n_p, n_r = size(group)
                rows, full, rest, loaded = (xs, x_full, x_rest, x3_in) if what == "x" else (pres, pre_full, pre_rest, pre_in)
                if n_p == P:
                    sp.dma_start(flat(rows[:, b]), full[:, bass.ds(group, 1), :].rearrange("p a f -> p (a f)")).then_inc(loaded[b], 16)
                else:
                    sp.dma_start(flat(rows[0:n_p, b, 0:n_r]), rest).then_inc(loaded[b], 16)

            def store3(group, turn, b):
                n_p, n_r = size(group)
                result = results[b % 2]
                if n_p == P:
                    sp.dma_start(out_full[:, bass.ds(group, 1), :].rearrange("p a f -> p (a f)"), flat(result)).then_inc(out_stored[b % 2], 16)
                else:
                    sp.dma_start(out_rest, flat(result[0:n_p, 0:n_r])).then_inc(out_stored[b % 2], 16)

            def nodes3(group, turn, b):
                sp.wait_ge(summed, group * 2 + 2)
                following = not isinstance(group, int) or group + SLOTS < GROUPS
                if following:
                    load3("x", group + SLOTS, b)
                store3(group, turn, b)
                if following:
                    load3("pre", group + SLOTS, b)
            for group in range(SLOTS):
                load3("x", group, group)
            sp.wait_ge(scattered, 32 * TILES)
            for group in range(SLOTS):
                load3("pre", group, group)
            over_groups3(sp, nodes3)
            for b in range(2):
                sp.wait_ge(out_stored[b], 16 * len(range(b, GROUPS, 2)))

        @block.gpsimd
        def _(pool):
            nc.gpsimd.memset(zeros, 0.0).then_inc(zeros_set, 1)
            pool.wait_ge(zeros_set, 1)
            for k in range(CLEARS_AHEAD):
                pool.dma_start(pre_by_p[:, k * CLEAR * H2:(k + 1) * CLEAR * H2], zeros).then_inc(pre_cleared[k], 16)
            nc.gpsimd.memset(ident[:], 0.0)
            nc.gpsimd.memset(earlier[:], 1.0)
            nc.gpsimd.iota(iota_i[:], pattern=[[P, 2]], base=0, channel_multiplier=1).then_inc(pool_self, 1)
            pool.wait_ge(pool_self, 1)
            nc.gpsimd.affine_select(out=ident[:], in_=ident[:], compare_op=ALU.not_equal, fill=1.0, base=0,
                                    pattern=[[-1, P]], channel_multiplier=1)
            nc.gpsimd.affine_select(out=earlier[:], in_=earlier[:], compare_op=ALU.is_gt, fill=0.0, base=0,
                                    pattern=[[-1, P]], channel_multiplier=1)
            nc.gpsimd.memset(ones[:], 1.0).then_inc(pool_const, 1)

            pool.dma_start(Wmsg[:, IN], W_in.rearrange("(c p) n -> p c n", p=P)).then_inc(weights_in, 16)
            pool.dma_start(Wmsg[:, OUT], W_out.rearrange("(c p) n -> p c n", p=P)).then_inc(weights_in, 16)
            for d in range(2):
                pool.dma_start(Wx[:, d], W_x2i[d * D:(d + 1) * D, :].rearrange("(c p) n -> p c n", p=P)).then_inc(weights_in, 16)
            pool.dma_start(Wh[:], W_h2h.rearrange("(c p) n -> p c n", p=P)).then_inc(weights_in, 16)
            for a, where in ((gamma, gb[:, 0]), (beta, gb[:, 1]), (b_in, bmsg[:, IN]), (b_out, bmsg[:, OUT])):
                for c in range(KC):
                    pool.dma_start(where[:, c:c + 1], a[c * P:(c + 1) * P].rearrange("(p o) -> p o", o=1)).then_inc(weights_in, 16)
            pool.dma_start(bx_row[:], b_x2i.rearrange("(o n) -> o n", o=1)).then_inc(weights_in, 16)

            with pool.Fori(1, CLEARS // CLEARS_AHEAD) as i:
                for k in range(CLEARS_AHEAD):
                    pool.wait_ge(pre_cleared[k], i * 16)
                    pool.dma_start(pre_by_p[:, bass.ds((i * CLEARS_AHEAD + k) * (CLEAR * H2), CLEAR * H2)],
                                   zeros).then_inc(pre_cleared[k], 16)
            for k, (r, n) in enumerate(REST_CLEARS):
                pool.dma_start(pre_by_p[:, r * H2:(r + n) * H2], zeros[:, 0:n * H2]).then_inc(rest_cleared, 16)

            GATHERS_AHEAD = SLOTS + 2

            def gather(t, b):
                before(pool, g_ready, t, SLOTS)
                nc.gpsimd.tensor_copy(gidx[:, b, :], gather_cols[:, bass.ds(t, 1), :].rearrange("p a d -> p (a d)")).then_inc(gidx_ready, 1)
                copied = value(pool, t + 1)
                pool.wait_ge(edge_tables, 1)
                pool.wait_ge(gidx_ready, copied)
                for d in range(2):
                    nc.gpsimd.indirect_dma_start(
                        out=xg[d][b], out_offset=None, in_=x,
                        in_offset=bass.IndirectOffsetOnAxis(ap=gidx[:, b, d:d + 1], axis=0)).then_inc(gathered[b], 16)

            def scatter(t, b):
                pool.wait_ge(rows_u_ready, t + 1)
                pool.wait_ge(pre_in_saved, t + 1)
                pool.wait_ge(pre_out_saved, t + 1)
                if is_first(t):
                    for k in range(CLEARS_AHEAD):
                        pool.wait_ge(pre_cleared[k], 16 * (CLEARS // CLEARS_AHEAD))
                    pool.wait_ge(rest_cleared, 16 * len(REST_CLEARS))
                else:
                    added = value(pool, t * 32)
                    pool.wait_ge(edge_tables, 1)
                    pool.wait_ge(scattered, added)
                for d in range(2):
                    nc.gpsimd.indirect_dma_start(
                        out=pre, out_offset=bass.IndirectOffsetOnAxis(ap=rows_u[d][b][:, 0:1], axis=0),
                        in_=pre_new[d][b][:, :], in_offset=None, compute_op=ALU.add).then_inc(scattered, 16)

            pool.wait_ge(edge_tables, 1)
            for t in range(GATHERS_AHEAD):
                gather(t, t % SLOTS)

            def tile(t, turn, b):
                scatter(t, b)
                if not (isinstance(t, int) and t + GATHERS_AHEAD >= TILES):
                    gather(t + GATHERS_AHEAD, (b + GATHERS_AHEAD) % SLOTS)
            over_tiles(pool, tile, tail=2)

            def scale_rows(p):
                pool.wait_ge(h3T_ready, p.index + 1)
                h = hs[0:p.parts, p.slot, p.j0:p.j1, :]
                nc.gpsimd.tensor_tensor(h, h, A_rows[0:p.parts, 0:p.rows, :], ALU.mult).then_inc(bn_scaled, 1)

            def shift_rows(p):
                pool.wait_ge(bn_scaled, p.index + 1)
                h = hs[0:p.parts, p.slot, p.j0:p.j1, :]
                nc.gpsimd.tensor_tensor(h, h, C_rows[0:p.parts, 0:p.rows, :], ALU.add).then_inc(bn_h_ready, 1)

            def finish(p):
                pool.wait_ge(mixed, p.index + 1)
                if p.q == 0:
                    before(pool, out_stored[p.slot % 2], p.turn * 2 + p.slot // 2, 1, 16)
                nc.gpsimd.tensor_tensor(results[p.slot % 2][0:p.parts, p.j0:p.j1, :], hs[0:p.parts, p.slot, p.j0:p.j1, :],
                                        xs[0:p.parts, p.slot, p.j0:p.j1, :], ALU.add).then_inc(summed, 1)

            def pair(p):
                if p.shifted(1).there:
                    scale_rows(p.shifted(1))
                if p.shifted(-3).there:
                    finish(p.shifted(-3))
                if p.shifted(1).there:
                    shift_rows(p.shifted(1))
            scale_rows(Pair(0, 0, 0, 0))
            shift_rows(Pair(0, 0, 0, 0))
            over_pairs(pool, pair)
            for k in (-2, -1, 0):
                finish(LAST.shifted(k))

        @block.scalar
        def _(act):
            act.wait_ge(pads_set, 1)
            act.wait_ge(M_ready, 2 * KC)
            def relu_rows(group, b, j0, j1):
                n_p, _ = size(group)
                for j in range(j0, j1):
                    ins = nc.scalar.activation(hs[0:n_p, b, j, :], xs[0:n_p, b, j, :], ACT.Relu,
                                               bias=ln_b[0:n_p, bass.ds(group, 1), j], scale=ln_r[0:n_p, bass.ds(group, 1), j])
                return ins

            def nodes1(group, turn, b):
                n_p, n_r = size(group)
                act.wait_ge(var_ready, group + 1)
                nc.scalar.activation(ln_std[0:n_p, b, 0:n_r], ln_mv[0:n_p, b, 0:n_r, 1], ACT.Sqrt,
                                     bias=eps_col[0:n_p, :]).then_inc(std_ready, 1)
                if not is_first(group):
                    relu1(group - 1, (b - 1) % SLOTS)

            def relu1(group, b):
                act.wait_ge(ln_ready, group + 1)
                before(act, hT_ready, group, SLOTS)
                relu_rows(group, b, 0, size(group)[1]).then_inc(h_ready, 1)
            over_groups(act, nodes1)
            relu1(GROUPS - 1, (GROUPS - 1) % SLOTS)

            act.wait_ge(bn_var, 1)
            nc.scalar.activation(bn_std[:], bn_mv[:, :, 1], ACT.Sqrt, bias=eps_col[:]).then_inc(bn_std_ready, 1)
            for k, (hi, lo) in enumerate(weight_parts):
                act.wait_ge(scaled_ready, k + 1)
                nc.scalar.copy(hi, scaled[k]).then_inc(weight_hi_ready, 1)

            def save_constant(k):
                act.wait_ge(vec_ready, k + 1)
                act.wait_ge(weight_lo_ready, k + 1)
                nc.scalar.mul(vec4[k][:, 0:D], vec_ps[k][0:4, 0:D], 0.5)
                nc.scalar.copy(vec4[k][:, D:H2], vec_ps[k][0:4, D:H2]).then_inc(halved_ready, 1)
                act.wait_ge(halved_ready, k + 1)
                nc.scalar.copy(const4[:, k, :], vec4[k]).then_inc(vec_saved, 1)

            def save_in(t, b):
                act.wait_ge(pre_in_ready, t + 1)
                before(act, scattered, t, SLOTS, 32)
                nc.scalar.copy(pre_new[IN][b][:, :], pre_ps[IN][b % 2][:, :]).then_inc(pre_in_saved, 1)
                before(act, pre_out_ready, t, 2)
                nc.scalar.copy(in_hi[:, b % 2, :], pre_ps[IN][b % 2][:, :]).then_inc(in_hi_ready, 1)

            def save_out(t, b):
                act.wait_ge(pre_out_ready, t + 1)
                before(act, scattered, t, SLOTS, 32)
                nc.scalar.copy(pre_new[OUT][b][:, :], pre_ps[OUT][b % 2][:, :]).then_inc(pre_out_saved, 1)

            def deviation(t, b):
                act.wait_ge(evar_ready, t + 1)
                nc.scalar.activation(e_std[:, b, :], e_mv[:, b, :, 1], ACT.Sqrt, bias=eps_col[:]).then_inc(estd_ready, 1)

            def relu(t, b):
                act.wait_ge(eln_ready, t + 1)
                before(act, gT_ready, t, SLOTS)
                for d in range(2):
                    ins = nc.scalar.activation(g[:, b, d, :], xg[d][b], ACT.Relu,
                                               bias=e_b[:, b, d:d + 1], scale=e_r[:, b, d:d + 1])
                ins.then_inc(g_ready, 1)

            def save_hi(t, b):
                act.wait_ge(gT_ready, t + 1)
                before(act, projected, t, SLOTS)
                nc.scalar.copy(gT_hi[:, b], gT_ps[b % 2])
                nc.scalar.copy(s_hi[:, b].rearrange("p d r -> p (d r)"), s_ps[b % 2]).then_inc(gT_hi_ready, 1)

            def tile(t, turn, b):
                more = not (isinstance(t, int) and t + 1 >= TILES)
                if more:
                    deviation(t + 1, (b + 1) % SLOTS)
                save_hi(t, b)
                if more:
                    relu(t + 1, (b + 1) % SLOTS)
                if not is_first(t):
                    save_in(t - 1, (b - 1) % SLOTS)
                if not (isinstance(t, int) and t < 2):
                    save_out(t - 2, (b - 2) % SLOTS)
            deviation(0, 0)
            relu(0, 0)
            for k in range(3):
                save_constant(k)
            act.wait_ge(rows_T, 1)
            for j in range(2):
                nc.scalar.copy(A_rows[:, j, :], rows_ps[:, 0:D])
                ins = nc.scalar.copy(C_rows[:, j, :], rows_ps[:, D:2 * D])
            ins.then_inc(rows_saved, 1)
            over_tiles(act, tile)
            save_in(TILES - 1, (TILES - 1) % SLOTS)
            save_out(TILES - 2, (TILES - 2) % SLOTS)
            save_out(TILES - 1, (TILES - 1) % SLOTS)

            def relu3(p):
                act.wait_ge(x3_in[p.slot], p.turn * 16 + 16)
                before(act, summed, p.index, 2 * SLOTS)
                relu_rows(p.group, p.slot, p.j0, p.j1).then_inc(h3_ready, 1)

            def save_hi3(p):
                act.wait_ge(h3T_ready, p.index + 1)
                before(act, own_ready, p.index, 4)
                nc.scalar.copy(hT_hi[:, p.buf, 0:p.rows, :, 0:p.parts], hT_ps3[p.buf][:, 0:p.rows, :, 0:p.parts]).then_inc(h3T_hi, 1)

            def tanh(p):
                act.wait_ge(gates_in, p.index + 1)
                gates = pres[0:p.parts, p.slot, p.j0:p.j1, :]
                nc.scalar.activation(gates, gates, ACT.Tanh).then_inc(gates_ready, 1)

            def pair(p):
                if p.shifted(1).there:
                    save_hi3(p.shifted(1))
                if p.shifted(2).there:
                    relu3(p.shifted(2))
                if p.shifted(-1).there:
                    tanh(p.shifted(-1))
            for k in range(2):
                relu3(Pair(0, 0, 0, 0).shifted(k))
            save_hi3(Pair(0, 0, 0, 0))
            over_pairs(act, pair)
            tanh(LAST)

        @block.vector
        def _(dve):
            v = nc.vector
            own = [0]

            def link(ins):
                own[0] += 1
                ins.then_inc(dve_self, 1)
                dve.wait_ge(dve_self, own[0])

            v.memset(eps_col[:], EPS).then_inc(pads_set, 1)
            v.memset(edge_rows_i[:], PAD_ROW)
            v.memset(edge_rows[:, 2:4], 0.0).then_inc(pads_set, 1)
            v.memset(ones_r[:].bitcast(F32), 1.0)
            dve.wait_ge(pool_const, 1)
            link(v.tensor_copy(dummy_rows[:], iota_i[:]))
            link(v.tensor_scalar(row_masks[:, 0:1], dummy_rows[:, 0:1], 2.0, None, ALU.is_ge))
            v.tensor_scalar(row_masks[:, 1:2], row_masks[:, 0:1], -1.0, None, ALU.mult)
            link(v.scalar_tensor_tensor(row_masks[:, 2:3], row_masks[:, 0:1], -2.0, dummy_rows[:, 0:1], ALU.mult, ALU.add))
            v.tensor_scalar(row_masks[:, 3:4], row_masks[:, 2:3], -2.0, 1.0, ALU.mult, ALU.add)
            link(v.tensor_scalar(dummy_rows[:], dummy_rows[:], float(DUMMY), None, ALU.add))
            dve.wait_ge(edges_in, 12 * 16)
            v.tensor_copy(edge_rows[:, 0:2], edge_rows_i[:]).then_inc(rows_ready, 1)
            for blk in range(2):
                w = (P, TILES - P)[blk]
                dve.wait_ge(edgeT_ready, blk + 1)
                link(v.tensor_copy(edge_cols[:, blk * P:blk * P + w, :].rearrange("p t k -> p k t"),
                                   bank[blk][:, :].rearrange("p (k t) -> p k t", k=4)[:, :, 0:w]))
            v.tensor_scalar(gather_cols[:, :, 0], edge_cols[:, :, 1], float(N - 1), None, ALU.min)
            v.tensor_scalar(gather_cols[:, :, 1], edge_cols[:, :, 0], float(N - 1), None, ALU.min).then_inc(edge_tables, 1)
            for d in range(2):
                dve.wait_ge(WT_ready, d + 1)
                v.tensor_copy(WmsgT[:, d], bank[2 + d][:, :].rearrange("p (c n) -> p c n", c=KC)).then_inc(WT_saved, 1)
            for d in range(2):
                for c in range(KC):
                    dve.wait_ge(M_ready, d * KC + c + 1)
                    v.tensor_copy(M[:, d, c, :], bank[4 + d * KC + c][:, :]).then_inc(M_saved, 1)

            def columns(group, b):
                n_p, n_r = size(group)
                dve.wait_ge(hT_ready, group + 1)
                for c in range(KC):
                    ins = v.bn_stats(col_stats[:, c, bass.ds(group, 1), :].rearrange("p a s -> p (a s)"), hT_ps1[b][c][:, 0:n_r * n_p])
                ins.then_inc(hT_used, 1)

            def factor(group, b):
                n_p, n_r = size(group)
                dve.wait_ge(std_ready, group + 1)
                v.reciprocal(ln_r[0:n_p, bass.ds(group, 1), 0:n_r].rearrange("p a j -> p (a j)"),
                             ln_std[0:n_p, b, 0:n_r]).then_inc(rstd_ready, 1)

            def offset(group, b):
                n_p, n_r = size(group)
                dve.wait_ge(rstd_ready, group + 1)
                v.scalar_tensor_tensor(ln_b[0:n_p, bass.ds(group, 1), 0:n_r].rearrange("p a j -> p (a j)"), ln_mv[0:n_p, b, 0:n_r, 0], -1.0,
                                       ln_r[0:n_p, bass.ds(group, 1), 0:n_r].rearrange("p a j -> p (a j)"), ALU.mult, ALU.mult).then_inc(ln_ready, 1)

            def nodes1(group, turn, b):
                n_p, n_r = size(group)
                last = (b - 1) % SLOTS
                dve.wait_ge(x_in[b], turn * 16 + 16)
                for j in range(n_r):
                    ins = v.bn_stats(ln_stats[0:n_p, b, j, :], xs[0:n_p, b, j, :])
                ins.then_inc(stats_ready, 1)
                if not is_first(group):
                    factor(group - 1, last)
                done = value(dve, group + 1)
                dve.wait_ge(pool_const, 1)
                dve.wait_ge(stats_ready, done)
                for j in range(n_r):
                    ins = v.bn_aggr(ln_mv[0:n_p, b, j, :], ln_stats[0:n_p, b, j, :])
                ins.then_inc(var_ready, 1)
                if not is_first(group):
                    offset(group - 1, last)
                if not (isinstance(group, int) and group < 3):
                    columns(group - 3, (b - 3) % SLOTS)
            over_groups(dve, nodes1)
            factor(GROUPS - 1, (GROUPS - 1) % SLOTS)
            offset(GROUPS - 1, (GROUPS - 1) % SLOTS)
            for group in range(GROUPS - 3, GROUPS):
                columns(group, group % SLOTS)
            dve.wait_ge(hT_used, GROUPS)

            def stage(t, b):
                v.tensor_copy(cols[:, b, :], edge_cols[:, bass.ds(t, 1), :].rearrange("p a k -> p (a k)")).then_inc(cols_ready, 1)
            for t in range(2):
                stage(t, t)

            for c in range(KC):
                ins = v.bn_aggr(bn_mv[:, c, :], col_stats[:, c].rearrange("p g s -> p (g s)"))
            ins.then_inc(bn_var, 1)
            dve.wait_ge(weights_in, 14 * 16)
            dve.wait_ge(bn_std_ready, 1)
            link(v.reciprocal(bn_rstd[:], bn_std[:]))
            link(v.tensor_tensor(bn_A[:], gb[:, 0], bn_rstd[:], ALU.mult))
            link(v.tensor_tensor(bn_t[:], bn_mv[:, :, 0], bn_A[:], ALU.mult))
            link(v.tensor_tensor(bn_C[:], gb[:, 1], bn_t[:], ALU.subtract))
            for c in range(KC):
                for k, col in enumerate((bn_C[:, c:c + 1], bmsg[:, IN, c:c + 1], bmsg[:, OUT, c:c + 1])):
                    v.tensor_scalar(col4[:, k, c, :], ones[:, 0:4], col, None, ALU.mult)
                v.tensor_scalar(rep[:, 0, c, :], ones[:], bn_A[:, c:c + 1], None, ALU.mult)
                ins = v.tensor_scalar(rep[:, 1, c, :], ones[:], bn_C[:, c:c + 1], None, ALU.mult)
            ins.then_inc(bn_cols_ready, 1)

            for k, raw in enumerate(weights):
                c = k // 3
                v.tensor_scalar(scaled[k][:, 0:D], raw[:, 0:D], bn_A[:, c:c + 1], 0.5, ALU.mult, ALU.mult)
                v.tensor_scalar(scaled[k][:, D:H2], raw[:, D:H2], bn_A[:, c:c + 1], None, ALU.mult).then_inc(scaled_ready, 1)
            for k, (hi, lo) in enumerate(weight_parts):
                dve.wait_ge(weight_hi_ready, k + 1)
                v.tensor_tensor(lo, scaled[k], hi.bitcast(F32), ALU.subtract).then_inc(weight_lo_ready, 1)

            def constant(k):
                dve.wait_ge(vec_saved, k + 1)
                link(v.tensor_scalar(spare4, const4[:, k, :].bitcast(F32), row_masks[0:4, 3:4], None, ALU.mult))
                return v.scalar_tensor_tensor(const4[:, k, :], vec4[k], row_masks[0:4, 2:3], spare4, ALU.mult, ALU.add)

            def save_lo(t, b):
                dve.wait_ge(gT_hi_ready, t + 1)
                v.tensor_tensor(gT_lo[:, b], gT_ps[b % 2], gT_hi[:, b].bitcast(F32), ALU.subtract)
                v.scalar_tensor_tensor(s4[:, b].rearrange("p d r -> p (d r)"),
                                       s_hi[:, b].bitcast(F32).rearrange("p d r -> p (d r)"), row_masks[0:4, 1:2],
                                       s_ps[b % 2], ALU.mult, ALU.add).then_inc(gT_lo_ready, 1)

            def split_in(t, b):
                dve.wait_ge(pre_in_saved, t + 1)
                dve.wait_ge(in_hi_ready, t + 1)
                before(dve, pre_out_ready, t, 2)
                v.tensor_tensor(in_lo[:, b % 2, :], pre_new[IN][b], in_hi[:, b % 2, :].bitcast(F32), ALU.subtract).then_inc(in_lo_ready, 1)

            def front(t, turn, b, done, splitting):
                nodes = idx_ps[b % 2]
                dve.wait_ge(gathered[b], turn * 32 + 32)
                for d in range(2):
                    ins = v.bn_stats(e_stats[:, b, d, :], xg[d][b])
                ins.then_inc(estats_ready, 1)
                if splitting:
                    split_in(*splitting)
                value_t = value(dve, t + 1)
                dve.wait_ge(pool_const, 1)
                dve.wait_ge(estats_ready, value_t)
                for d in range(2):
                    ins = v.bn_aggr(e_mv[:, b, d, :], e_stats[:, b, d, :])
                ins.then_inc(evar_ready, 1)
                dve.wait_ge(cols_ready, t + 1)
                dve.wait_ge(idxT_ready, t + 1)
                v.tensor_tensor(shift[:, b, :], dummy_rows[:], cols[:, b, 0:2], ALU.subtract)
                for d in range(2):
                    ins = v.scalar_tensor_tensor(junk[:, d, :], nodes[:, d, :], cols[:, b, d:d + 1], earlier[:],
                                                 ALU.is_equal, ALU.mult, accum_out=dups[:, b, d:d + 1])
                ins.then_inc(dups_ready, 1)
                before(dve, gT_ready, t, SLOTS)
                v.tensor_scalar(merge[:, b, IN, :], nodes[:, IN, :], cols[:, b, IN:IN + 1], cols[:, b, 2 + IN:3 + IN],
                                ALU.is_equal, ALU.mult)
                dve.wait_ge(dups_ready, t + 1)
                v.scalar_tensor_tensor(kept[:, b, :], dups[:, b, :], 0.0, shift[:, b, :], ALU.is_gt, ALU.mult).then_inc(kept_ready, 1)
                dve.wait_ge(estd_ready, t + 1)
                v.reciprocal(e_r[:, b, :], e_std[:, b, :]).then_inc(erstd_ready, 1)
                dve.wait_ge(kept_ready, t + 1)
                v.tensor_tensor(rows_f[:, b, :], kept[:, b, :], cols[:, b, 0:2], ALU.add).then_inc(rows_f_ready, 1)
                v.tensor_scalar(merge[:, b, OUT, :], nodes[:, OUT, :], cols[:, b, OUT:OUT + 1], cols[:, b, 2 + OUT:3 + OUT],
                                ALU.is_equal, ALU.mult).then_inc(merge_ready, 1)
                dve.wait_ge(erstd_ready, t + 1)
                v.scalar_tensor_tensor(e_b[:, b, :], e_mv[:, b, :, 0], -1.0, e_r[:, b, :], ALU.mult, ALU.mult).then_inc(eln_ready, 1)
                before(dve, pre_out_ready, t, SLOTS)
                dve.wait_ge(rows_f_ready, t + 1)
                v.scalar_tensor_tensor(cross[:, b, :], nodes[:, OUT, :], rows_f[:, b, IN:IN + 1], ones[:],
                                       ALU.is_equal, ALU.mult, accum_out=taken[:, b, :]).then_inc(cross_ready, 1)
                v.tensor_tensor(to_dummy[:, b, :], dummy_rows[:, 0:1], rows_f[:, b, 0:1], ALU.subtract).then_inc(to_dummy_ready, 1)
                if done:
                    name_rows(*done)
                dve.wait_ge(cross_ready, t + 1)
                dve.wait_ge(to_dummy_ready, t + 1)
                v.scalar_tensor_tensor(moved[:, b, :], taken[:, b, :], 0.0, to_dummy[:, b, :], ALU.is_gt, ALU.mult).then_inc(moved_ready, 1)

            def name_rows(t, b):
                before(dve, scattered, t, SLOTS, 32)
                v.tensor_copy(rows_u[OUT][b][:], rows_f[:, b, OUT:OUT + 1])
                dve.wait_ge(moved_ready, t + 1)
                v.tensor_tensor(rows_u[IN][b][:], moved[:, b, :], rows_f[:, b, IN:IN + 1], ALU.add).then_inc(rows_u_ready, 1)

            def tile(t, turn, b):
                splitting = None if isinstance(t, int) and t < 2 else (t - 2, (b - 2) % SLOTS)
                if not (isinstance(t, int) and t + 2 >= TILES):
                    stage(t + 2, (b + 2) % SLOTS)
                if not (isinstance(t, int) and t + 1 >= TILES):
                    front(t + 1, turn + (b + 1) // SLOTS, (b + 1) % SLOTS, (t, b), splitting)
                else:
                    split_in(*splitting)
                    name_rows(t, b)
                save_lo(t, b)
            front(0, 0, 0, None, None)
            link(constant(IN))
            link(constant(OUT))
            constant(2).then_inc(spare_used, 1)
            over_tiles(dve, tile)
            for t in (TILES - 2, TILES - 1):
                split_in(t, t % SLOTS)

            def save_lo3(p):
                dve.wait_ge(h3T_hi, p.index + 1)
                v.tensor_tensor(hT_lo[:, p.buf, 0:p.rows, :, 0:p.parts], hT_ps3[p.buf][:, 0:p.rows, :, 0:p.parts],
                                hT_hi[:, p.buf, 0:p.rows, :, 0:p.parts].bitcast(F32), ALU.subtract).then_inc(h3T_lo, 1)

            def add_own(p, j):
                sums = pres[0:p.parts, p.slot, j, :]
                return v.tensor_tensor(sums, sums, node_ps[j][0:p.parts, :], ALU.add)

            def operands(p):
                rows = pres[0:p.parts, p.slot, p.j0:p.j1, :]
                return hs[0:p.parts, p.slot, p.j0:p.j1, :], rows[:, :, 0:D], rows[:, :, D:H2]

            def mix_a(p):
                h, _, new = operands(p)
                dve.wait_ge(gates_ready, p.index + 1)
                dve.wait_ge(bn_h_ready, p.index + 1)
                v.tensor_tensor(h, h, new, ALU.subtract).then_inc(diff_ready, 1)

            def mix_b(p):
                h, gate, _ = operands(p)
                dve.wait_ge(diff_ready, p.index + 1)
                v.scalar_tensor_tensor(h, gate, 1.0, h, ALU.add, ALU.mult).then_inc(gated_ready, 1)

            def mix_c(p):
                h, _, new = operands(p)
                dve.wait_ge(gated_ready, p.index + 1)
                v.scalar_tensor_tensor(h, h, 0.5, new, ALU.mult, ALU.add).then_inc(mixed, 1)

            def steps(splitting, adding, mixing):
                if adding:
                    if adding.q == 0:
                        dve.wait_ge(pre_in[adding.slot], adding.turn * 16 + 16)
                    dve.wait_ge(own_ready, adding.index + 1)
                    ins = add_own(adding, adding.j0)
                    if adding.rows == 1:
                        ins.then_inc(gates_in, 1)
                if mixing:
                    mix_a(mixing)
                if adding and adding.rows == 2:
                    add_own(adding, adding.j0 + 1).then_inc(gates_in, 1)
                if mixing:
                    mix_b(mixing)
                if splitting:
                    save_lo3(splitting)
                if mixing:
                    mix_c(mixing)

            def pair(p):
                steps(*(p.shifted(k) if p.shifted(k).there else None for k in (1, -1, -2)))
            save_lo3(Pair(0, 0, 0, 0))
            over_pairs(dve, pair)
            steps(None, LAST, LAST.shifted(-1))
            steps(None, None, LAST)

        @block.tensor
        def _(pe):
            mm, transpose = nc.tensor.matmul, nc.tensor.transpose
            pe.wait_ge(pool_const, 1)
            pe.wait_ge(rows_ready, 1)
            for blk in range(2):
                w = (P, TILES - P)[blk]
                for k in range(4):
                    ins = transpose(bank[blk][:, k * P:k * P + w], edge_rows[0:w, k, blk, :], ident[0:w, 0:w])
                ins.then_inc(edgeT_ready, 1)
            pe.wait_ge(weights_in, 14 * 16)
            for d in range(2):
                for c2 in range(KC):
                    for c1 in range(KC):
                        ins = transpose(bank[2 + d][:, c2 * D + c1 * P:c2 * D + (c1 + 1) * P],
                                        Wmsg[:, d, c1, c2 * P:(c2 + 1) * P], ident[:])
                ins.then_inc(WT_ready, 1)
            for d in range(2):
                pe.wait_ge(WT_saved, d + 1)
                for c1 in range(KC):
                    for c2 in range(KC):
                        ins = mm(bank[4 + d * KC + c1][:, :], WmsgT[:, d, c2, c1 * P:(c1 + 1) * P], Wx[:, d, c2, :],
                                 start=(c2 == 0), stop=(c2 == KC - 1))
                    ins.then_inc(M_ready, 1)

            pe.wait_ge(edge_tables, 1)
            pe.wait_ge(M_saved, 2 * KC)

            def nodes1(group, turn, b):
                n_p, n_r = size(group)
                pe.wait_ge(h_ready, group + 1)
                before(pe, hT_used, group, SLOTS)
                for c in range(KC):
                    for j in range(n_r):
                        ins = transpose(hT_ps1[b][c][:, j * n_p:(j + 1) * n_p], hs[0:n_p, b, j, c * P:(c + 1) * P],
                                        ident[0:n_p, 0:n_p])
                ins.then_inc(hT_ready, 1)
            over_groups(pe, nodes1)

            def spread_indices(t, b):
                pe.wait_ge(cols_ready, t + 1)
                before(pe, gT_lo_ready, t, 2)
                for d in range(2):
                    ins = transpose(idx_ps[b % 2][:, d, :], cols[:, b, d:d + 1].to_broadcast([P, P]), ident[:])
                ins.then_inc(idxT_ready, 1)

            pe.wait_ge(bn_cols_ready, 1)
            spread_indices(0, 0)
            for d in range(2):
                for c in range(KC):
                    mm(vec_ps[d][0:4, :], col4[:, 0, c, :], M[:, d, c, :], start=(c == 0), stop=False)
                for c in range(KC):
                    ins = mm(vec_ps[d][0:4, :], col4[:, 1 + d, c, :], Wx[:, d, c, :], start=False, stop=(c == KC - 1))
                ins.then_inc(vec_ready, 1)
            for c in range(KC):
                mm(vec_ps[2][0:4, :], col4[:, 0, c, :], Wh[:, c, :], start=(c == 0), stop=False)
            mm(vec_ps[2][0:4, :], ones[0:1, 0:4], bx_row[:], start=False, stop=True).then_inc(vec_ready, 1)
            for k in range(2):
                for c in range(KC):
                    ins = transpose(rows_ps[:, k * D + c * P:k * D + (c + 1) * P], rep[:, k, c, :], ident[:])
            ins.then_inc(rows_T, 1)

            def exact3(to, left_hi, left_lo, right_hi, right_lo, first, last):
                mm(to, left_hi, right_hi, start=first, stop=False)
                mm(to, left_hi, right_lo, start=False, stop=False)
                return mm(to, left_lo, right_hi, start=False, stop=last)

            def merge_rows(t, b):
                pe.wait_ge(g_ready, t + 1)
                pe.wait_ge(merge_ready, t + 1)
                before(pe, gT_lo_ready, t, 2)
                for d in range(2):
                    for c in range(KC):
                        mm(gT_ps[b % 2][:, d, c, :], g[:, b, d, c * P:(c + 1) * P], merge[:, b, d, :], start=True, stop=True)
                pe.wait_ge(cross_ready, t + 1)
                mm(s_ps[b % 2], ones[:, 0:4], merge[:, b].rearrange("p d r -> p (d r)"),
                   start=True, stop=True).then_inc(gT_ready, 1)

            def project(t, b, d):
                pe.wait_ge(gT_lo_ready, t + 1)
                if is_first(t):
                    pe.wait_ge(weight_lo_ready, 2 * KC + KC)
                    pe.wait_ge(spare_used, 1)
                    pe.wait_ge(rows_saved, 1)
                if d == IN:
                    before(pe, in_hi_ready, t, 2)
                else:
                    before(pe, pre_out_saved, t, 2)
                to = pre_ps[d][b % 2][:, :]
                for c in range(KC):
                    exact3(to, gT_hi[:, b, d, c, :], gT_lo[:, b, d, c, :], M_hi[:, d, c, :], M_lo[:, d, c, :], c == 0, False)
                ins = mm(to, s4[:, b, d, :], const4[:, d, :], start=False, stop=(d == IN))
                ins.then_inc(pre_in_ready if d == IN else projected, 1)

            def add_cross(t, b):
                pe.wait_ge(in_lo_ready, t + 1)
                pe.wait_ge(cross_ready, t + 1)
                mm(pre_ps[OUT][b % 2][:, :], cross[:, b, :], in_hi[:, b % 2, :], start=False, stop=False)
                mm(pre_ps[OUT][b % 2][:, :], cross[:, b, :], in_lo[:, b % 2, :], start=False, stop=True).then_inc(pre_out_ready, 1)

            def tile(t, turn, b):
                if not (isinstance(t, int) and t + 1 >= TILES):
                    spread_indices(t + 1, (b + 1) % SLOTS)
                merge_rows(t, b)
                if not is_first(t):
                    project(t - 1, (b - 1) % SLOTS, IN)
                if not (isinstance(t, int) and t < 2):
                    add_cross(t - 2, (b - 2) % SLOTS)
                if not is_first(t):
                    project(t - 1, (b - 1) % SLOTS, OUT)
            over_tiles(pe, tile)
            project(TILES - 1, (TILES - 1) % SLOTS, IN)
            add_cross(TILES - 2, (TILES - 2) % SLOTS)
            project(TILES - 1, (TILES - 1) % SLOTS, OUT)
            add_cross(TILES - 1, (TILES - 1) % SLOTS)

            pe.wait_ge(gT_lo_ready, TILES)
            pe.wait_ge(pre_out_saved, TILES)

            def transpose_pair(p):
                pe.wait_ge(h3_ready, p.index + 1)
                before(pe, h3T_lo, p.index, 4)
                for j in range(p.j0, p.j1):
                    for c in range(KC):
                        ins = transpose(hT_ps3[p.buf][:, j - p.j0, c, 0:p.parts], hs[0:p.parts, p.slot, j, c * P:(c + 1) * P],
                                        ident[0:p.parts, 0:p.parts])
                ins.then_inc(h3T_ready, 1)

            def own_product(p):
                pe.wait_ge(h3T_lo, p.index + 1)
                before(pe, gates_in, p.index, 2)
                for j in range(p.j0, p.j1):
                    to = node_ps[j][0:p.parts, :]
                    mm(to, ones_r[0:2, 0:p.parts], const4[0:2, 2, :], start=True, stop=False)
                    for c in range(KC):
                        ins = exact3(to, hT_hi[:, p.buf, j - p.j0, c, 0:p.parts], hT_lo[:, p.buf, j - p.j0, c, 0:p.parts],
                                     Wh_hi[:, c, :], Wh_lo[:, c, :], False, c == KC - 1)
                ins.then_inc(own_ready, 1)

            def pair(p):
                if p.shifted(1).there:
                    transpose_pair(p.shifted(1))
                own_product(p)
            for k in range(1):
                transpose_pair(Pair(0, 0, 0, 0).shifted(k))
            over_pairs(pe, pair)


INPUTS = ["x", "src", "dst", "edge_weight", "edge_weight_n2", "L0_gnn_gamma", "L0_gnn_beta", "L0_gnn_W_in", "L0_gnn_b_in",
          "L0_gnn_W_out", "L0_gnn_b_out", "L0_gnn_W_x2i", "L0_gnn_b_x2i", "L0_gnn_W_h2h"]


def kernel(**inputs):
    import concourse.bacc as bacc
    from concourse.bass_utils import run_bass_kernel_spmd

    nc = bacc.Bacc("TRN2", target_bir_lowering=False, num_devices=1)
    arrays, aps = {}, []
    for name in INPUTS:
        a = np.ascontiguousarray(inputs[name])
        arrays[f"in_{name}"] = a
        aps.append(nc.dram_tensor(f"in_{name}", a.shape, mybir.dt.from_np(a.dtype), kind="ExternalInput").ap())
    x = inputs["x"]
    out = nc.dram_tensor("out", x.shape, F32, kind="ExternalOutput").ap()
    build(nc, *aps, out)
    r = run_bass_kernel_spmd(nc, [arrays], core_ids=[0])
    return r.results[0]["out"]
```
